# Optimizing a Trainium2 kernel written in Bass

```python
import numpy as np
import jax
import jax.numpy as jnp

def _softmax(x, axis=-1):
    return jax.nn.softmax(x, axis=axis)

def _gelu(x):
    return jax.nn.gelu(x, approximate=True)

def _silu(x):
    return jax.nn.silu(x)

def _sigmoid(x):
    return jax.nn.sigmoid(x)

def _layernorm(x, axis=-1, eps=1e-05):
    m = jnp.mean(x, axis=axis, keepdims=True)
    v = jnp.var(x, axis=axis, keepdims=True)
    return (x - m) / jnp.sqrt(v + eps)

def _scatter_add(tgt, idx, src, axis=0):
    return tgt.at[idx].add(src)

def _segment_sum(src, seg, n):
    return jax.ops.segment_sum(src, seg, n)
kernel_name = 'mk_xattn_seq_d1_seqx_r4_2e50fa'

def setup_inputs(seed: int=0):
    np.random.seed(seed)
    _w = jnp.asarray

    def _rec_inputs():
        import jax
        import jax.numpy as jnp
        _rk = jax.random.key(seed)
        x = -0.000125 + 0.9999 * jax.random.normal(jax.random.fold_in(_rk, 1), (8, 512, 512), jnp.float32)
        _lenS = 512 - jax.random.randint(jax.random.fold_in(_rk, 7), (8,), 0, max(1, 512 // 4) + 1, jnp.int32)
        _lenS2 = 1601 - jax.random.randint(jax.random.fold_in(_rk, 8), (8,), 0, max(1, 1601 // 4) + 1, jnp.int32)
        _ctx_1024P = jax.random.normal(jax.random.fold_in(_rk, 11), (8, 16, 256), jnp.float32)
        _ctx_1024c = jax.random.dirichlet(jax.random.fold_in(_rk, 511), 0.3 * jnp.ones((16,), jnp.float32), (8, 1601))
        _ctx_1024t = jnp.einsum('bsk,bkd->bsd', _ctx_1024c, _ctx_1024P)
        _ctx_1024t = _ctx_1024t * jax.lax.rsqrt(jnp.mean(jnp.square(_ctx_1024t)) + 1e-12) * 0.953939
        ctx_1024 = 4.13588e-05 + 0.999923 * (_ctx_1024t + 0.3 * jax.random.normal(jax.random.fold_in(_rk, 611), (8, 1601, 256), jnp.float32))
        return (x, ctx_1024)
    x, ctx_1024 = _rec_inputs()

    def _L0_xattn_setup():
        import jax, jax.numpy as jnp
        import numpy as np
        EPS = 1e-06

        def _rmsnorm(x, w):
            var = jnp.mean(jnp.square(x), axis=-1, keepdims=True)
            return x * jax.lax.rsqrt(var + EPS) * w
        key = jax.random.key(seed)
        ks = jax.random.split(key, 6)
        B, N, M = (4, 1024, 512)
        d_model, memory_dim = (512, 256)
        hidden_states = jax.random.normal(ks[0], (B, N, d_model), dtype=jnp.float32)
        memory = jax.random.normal(ks[1], (B, M, memory_dim), dtype=jnp.float32)
        W_mem = jax.random.normal(ks[2], (d_model, memory_dim), dtype=jnp.float32) / np.sqrt(memory_dim)
        W_gate = jax.random.normal(ks[3], (d_model, 2 * d_model), dtype=jnp.float32) / np.sqrt(2 * d_model)
        b_gate = jax.random.normal(ks[4], (d_model,), dtype=jnp.float32) * 0.01
        norm_w = jnp.ones((d_model,), dtype=jnp.float32)
        return {'hidden_states': hidden_states, 'memory': memory, 'W_mem': W_mem, 'W_gate': W_gate, 'b_gate': b_gate, 'norm_w': norm_w}
    _L0_xattn_all = _L0_xattn_setup()
    _L0_xattn_in = {k: v for k, v in _L0_xattn_all.items() if k in ('W_mem', 'W_gate', 'b_gate', 'norm_w')}
    del _L0_xattn_all
    return {'x': x, 'ctx_1024': ctx_1024, 'L0_xattn_W_mem': _L0_xattn_in['W_mem'], 'L0_xattn_W_gate': _L0_xattn_in['W_gate'], 'L0_xattn_b_gate': _L0_xattn_in['b_gate'], 'L0_xattn_norm_w': _L0_xattn_in['norm_w']}

def reference(x, ctx_1024, L0_xattn_W_mem, L0_xattn_W_gate, L0_xattn_b_gate, L0_xattn_norm_w):
    import jax
    import jax.numpy as jnp

    def _L0_xattn_ref(hidden_states, memory, W_mem, W_gate, b_gate, norm_w):
        import jax, jax.numpy as jnp
        import numpy as np
        EPS = 1e-06

        def _rmsnorm(x, w):
            var = jnp.mean(jnp.square(x), axis=-1, keepdims=True)
            return x * jax.lax.rsqrt(var + EPS) * w
        D = hidden_states.shape[-1]
        memory_proj = jnp.einsum('bme,de->bmd', memory, W_mem)
        scores = jnp.einsum('bnd,bmd->bnm', hidden_states, memory_proj) / jnp.sqrt(jnp.float32(D))
        attn = jax.nn.softmax(scores, axis=-1)
        memory_context = jnp.einsum('bnm,bmd->bnd', attn, memory_proj)
        gate_input = jnp.concatenate([hidden_states, memory_context], axis=-1)
        gate = jax.nn.sigmoid(jnp.einsum('bnf,df->bnd', gate_input, W_gate) + b_gate)
        fused = hidden_states + gate * memory_context
        return _rmsnorm(fused, norm_w)
    x = _L0_xattn_ref(x, ctx_1024, L0_xattn_W_mem, L0_xattn_W_gate, L0_xattn_b_gate, L0_xattn_norm_w)
    return x

_drawn_inputs = setup_inputs


def setup_inputs(seed=0):
    import zlib

    import numpy as np

    out = dict(_drawn_inputs(seed))
    spreads = {'L0_xattn_norm_w': (1.0, 0.2)}
    factors = {'L0_xattn_b_gate': 51.813}
    for name, (base, spread) in spreads.items():
        noise = np.random.default_rng([zlib.crc32(name.encode()), seed]).standard_normal(out[name].shape)
        drawn = base * np.exp(spread * noise) if base else spread * noise
        out[name] = jnp.asarray(drawn.astype(out[name].dtype))
    for name, factor in factors.items():
        out[name] = (out[name] * factor).astype(out[name].dtype)
    return out
```

```python
from contextlib import ExitStack

import concourse.bass as bass
from concourse import mybir

ALU = mybir.AluOpType
ACT = mybir.ActivationFunctionType
AX = mybir.AxisListType
F32 = mybir.dt.float32
F32R = mybir.dt.float32r
I32 = mybir.dt.int32

P = 128
EPS = 1e-6
RSQRT_MAGIC = float(0x5F3759DF)
NEWTON_STEPS = 3


def xattn_kernel(nc: bass.Bass, x, mem, w, wg, b_gate, norm_w, out):
    B, N, D = x.shape
    _, M, C = mem.shape
    NT = N // P
    DT = D // P
    CT = C // P
    MT = -(-M // P)
    LAST = M - (MT - 1) * P
    MP = -(-MT // 2)
    TMP_RING = 4
    LO_RING = 6
    assert N == 512 and D == 512 and C == 256 and MT % 2 == 1

    def rows(t):
        return P if t < MT - 1 else LAST

    with ExitStack() as ctx:

        def sb(name, shape, dt=F32):
            return ctx.enter_context(nc.sbuf_tensor(name, shape, dt))

        def sem(name):
            return ctx.enter_context(nc.semaphore(name))

        s_offset = -(-nc.sbuf_base // 32) * 32
        s = sb("s", [P, MT, N])
        p_hi = nc.alloc_sbuf_tensor_at("p_hi", [P, MT, N], F32R, offset=s_offset)
        p_tmp = sb("p_tmp", [P, TMP_RING, N])
        p_lo = sb("p_lo", [P, LO_RING, N], F32R)
        mem_raw = sb("mem_raw", [P, MT, C])
        mem_hi = sb("mem_hi", [P, MT, C], F32R)
        mem_lo = sb("mem_lo", [P, MT, C], F32R)
        mt_hi = sb("mt_hi", [P, 2, CT, 2 * P], F32R)
        mt_lo = sb("mt_lo", [P, 2, CT, 2 * P], F32R)
        x_raw = sb("x_raw", [P, NT, D])
        xt_hi = sb("xt_hi", [P, DT, N], F32R)
        xt_lo = sb("xt_lo", [P, DT, N], F32R)
        q_hi = sb("q_hi", [P, CT, N], F32R)
        q_lo = sb("q_lo", [P, CT, N], F32R)
        u_hi = sb("u_hi", [P, CT, N], F32R)
        u_lo = sb("u_lo", [P, CT, N], F32R)
        gate = sb("gate", [P, NT, D])
        fused = sb("fused", [P, NT, D])
        x_again = sb("x_again", [P, 2, D])
        w_hi = sb("w_hi", [P, DT, C], F32R)
        w_lo = sb("w_lo", [P, DT, C], F32R)
        wt_hi = sb("wt_hi", [P, CT, D], F32R)
        wt_lo = sb("wt_lo", [P, CT, D], F32R)
        wg1t_hi = sb("wg1t_hi", [P, DT, D], F32R)
        wg1t_lo = sb("wg1t_lo", [P, DT, D], F32R)
        v_hi = sb("v_hi", [P, CT, D], F32R)
        v_lo = sb("v_lo", [P, CT, D], F32R)
        bias_rows = sb("bias_rows", [P, D])
        norm_rows = sb("norm_rows", [P, D])
        run = sb("run", [P, N])
        max_rows = sb("max_rows", [P, N])
        psum_rows = sb("psum_rows", [P, N])
        diag = sb("diag", [P, NT, P])
        ident = sb("ident", [P, P])
        ones = sb("ones", [P, P])
        col_max = sb("col_max", [P, NT])
        r_sum = sb("r_sum", [P, NT])
        r_half = sb("r_half", [P, NT])
        sq_sum = sb("sq_sum", [P, NT])
        mean_sq = sb("mean_sq", [P, NT])
        r_rms = sb("r_rms", [P, NT])
        nw_a = sb("nw_a", [P, NT])
        nw_b = sb("nw_b", [P, NT])
        w_raw = x_again[:, :, :].rearrange("p a (k c) -> p (a k) c", c=C)
        wg_raw = [
            (gate, fused)[i // 2][:, 2 * (i % 2) : 2 * (i % 2) + 2, :].rearrange("p a f -> p (a f)")
            for i in range(DT)
        ]

        bank = [ctx.enter_context(nc.psum_tensor(f"bank{i}", [P, 512], F32)) for i in range(8)]
        U_BANK, S_BANK, G_BANK, CTX_BANK = 0, 2, 4, 6

        def s_bank(t):
            return bank[S_BANK + t % 3]

        def mt_bank(p):
            return bank[5 + p % 2]

        in_x, in_w, in_wg, in_rows = sem("in_x"), sem("in_w"), sem("in_wg"), sem("in_rows")
        in_mem = [sem(f"in_mem{p}") for p in range(MP)]
        in_x_again = [sem(f"in_x_again{i}") for i in range(2)]
        stored = [sem(f"stored{j}") for j in range(NT)]
        cleared, ready_ident, ready_ones, ready_pad = (
            sem("cleared"), sem("ready_ident"), sem("ready_ones"), sem("ready_pad"))
        w_split_hi, w_split_lo = sem("w_split_hi"), sem("w_split_lo")
        pe_wt, wt_split_hi, wt_split_lo = sem("pe_wt"), sem("wt_split_hi"), sem("wt_split_lo")
        pe_mt, pe_s, pe_max_t, pe_max_rows = sem("pe_mt"), sem("pe_s"), sem("pe_max_t"), sem("pe_max_rows")
        pe_sum, pe_ctx, pe_g, pe_gx = sem("pe_sum"), sem("pe_ctx"), sem("pe_g"), sem("pe_gx")
        pe_xt, pe_q, pe_u = sem("pe_xt"), sem("pe_q"), sem("pe_u")
        s_copied, mt_has_hi, mem_has_hi = sem("s_copied"), sem("mt_has_hi"), sem("mem_has_hi")
        exp_done, p_has_hi, xt_has_hi = sem("exp_done"), sem("p_has_hi"), sem("xt_has_hi")
        q_has_hi, u_has_hi, max_copied = sem("q_has_hi"), sem("u_has_hi"), sem("max_copied")
        ctx_copied, tanh_done, squares_done = sem("ctx_copied"), sem("tanh_done"), sem("squares_done")
        run_done, mt_has_lo, mem_has_lo = sem("run_done"), sem("mt_has_lo"), sem("mem_has_lo")
        col_max_done, diag_done, shifted = sem("col_max_done"), sem("diag_done"), sem("shifted")
        p_has_lo, xt_has_lo, q_has_lo = sem("p_has_lo"), sem("xt_has_lo"), sem("q_has_lo")
        u_has_lo, gx_done, r_first, r_done = sem("u_has_lo"), sem("gx_done"), sem("r_first"), sem("r_done")
        z_done, gated, fused_done = sem("z_done"), sem("gated"), sem("fused_done")
        newton, out_done = sem("newton"), sem("out_done")
        p_added = sem("p_added")

        NEWTON_OPS = 2 + 3 * NEWTON_STEPS
        WG1T, WG2T, WT, V = range(0, 4), range(4, 8), range(8, 10), range(10, 12)

        X_AT = [6, 7, 9, 11]

        def weight_bank(g):
            return bank[4 + g % 4]

        block = ctx.enter_context(nc.Block())

        @block.sync
        def _(sp):
            def load_x(b):
                sp.dma_start(x_raw[:, :, :], x[b].rearrange("(t p) d -> p t d", p=P)).then_inc(in_x, 16)

            def load_mem(b, p):
                if p < MP - 1:
                    src = mem[b, 2 * p * P : (2 * p + 2) * P, :].rearrange("(t p) c -> p t c", p=P)
                    sp.dma_start(mem_raw[:, 2 * p : 2 * p + 2, :], src).then_inc(in_mem[p], 16)
                else:
                    sp.dma_start(mem_raw[0:LAST, MT - 1, :], mem[b, (MT - 1) * P : M, :]).then_inc(in_mem[p], 16)

            def load_x_again(b, j):
                sp.dma_start(x_again[:, j % 2, :], x[b, j * P : (j + 1) * P, :]).then_inc(in_x_again[j % 2], 16)

            def store(b, j):
                sp.wait_ge(out_done, NT * b + j + 1)
                sp.dma_start(out[b, j * P : (j + 1) * P, :], fused[:, j, :]).then_inc(stored[j], 16)

            def finish_io(b):
                for j in range(2, NT):
                    sp.wait_ge(fused_done, NT * b + j - 1)
                    load_x_again(b, j)
                for j in range(NT):
                    store(b, j)

            def iteration(b, first, last):
                if not last:
                    sp.wait_ge(pe_xt, DT * (b + 1))
                    if first:
                        sp.wait_ge(pe_wt, V[-1] + 1)
                    load_x(b + 1)
                if not first:
                    sp.wait_ge(fused_done, NT * (b - 1))
                    load_x_again(b - 1, 0)
                    load_x_again(b - 1, 1)
                if not last:
                    for p in range(MP):
                        sp.wait_ge(pe_mt, MP * b + p + 1)
                        sp.wait_ge(mem_has_lo, MP * b + p + 1)
                        load_mem(b + 1, p)
                if not first:
                    finish_io(b - 1)

            load_x(0)
            sp.dma_start(w_raw, w.rearrange("(k p) c -> p k c", p=P)).then_inc(in_w, 16)
            load_mem(0, 0)
            load_mem(0, 1)
            load_mem(0, 2)
            for i in range(DT):
                sp.dma_start(wg_raw[i], wg[i * P : (i + 1) * P, :]).then_inc(in_wg, 16)
            sp.wait_ge(ready_pad, 1)
            for p in range(3, MP):
                load_mem(0, p)
            sp.dma_start(bias_rows[:, :], b_gate.partition_broadcast(P)).then_inc(in_rows, 16)
            sp.dma_start(norm_rows[:, :], norm_w.partition_broadcast(P)).then_inc(in_rows, 16)

            for p in range(MP):
                sp.wait_ge(pe_mt, p + 1)
                sp.wait_ge(mem_has_lo, p + 1)
                load_mem(1, p)
            sp.wait_ge(pe_wt, V[-1] + 1)
            load_x(1)
            with sp.Fori(1, B - 1) as b:
                iteration(b, False, False)
            iteration(B - 1, False, True)
            sp.wait_ge(fused_done, NT * (B - 1))
            load_x_again(B - 1, 0)
            load_x_again(B - 1, 1)
            finish_io(B - 1)
            for j in range(NT):
                sp.wait_ge(stored[j], 16 * B)

        @block.tensor
        def _(pe):
            def product(dst, terms):
                n = len(terms)
                for i, (a_hi, a_lo, b_hi, b_lo) in enumerate(terms):
                    nc.tensor.matmul(dst, a_hi, b_hi, start=(i == 0), stop=False)
                    nc.tensor.matmul(dst, a_hi, b_lo, start=False, stop=False)
                    last = nc.tensor.matmul(dst, a_lo, b_hi, start=False, stop=(i == n - 1))
                return last

            def transpose_x(b, k):
                if k >= 2:
                    pe.wait_ge(xt_has_lo, DT * b + k - 1)
                for j in range(NT):
                    last = nc.tensor.transpose(
                        bank[CTX_BANK + k % 2][:, j * P : (j + 1) * P], x_raw[:, j, k * P : (k + 1) * P], ident[:, :])
                last.then_inc(pe_xt, 1)

            def query(b, c):
                product(bank[S_BANK + c][:, :], [
                    (w_hi[:, k, c * P : (c + 1) * P], w_lo[:, k, c * P : (c + 1) * P], xt_hi[:, k, :], xt_lo[:, k, :])
                    for k in range(DT)]).then_inc(pe_q, 1)

            def transpose_mem(b, p):
                pe.wait_ge(in_mem[p], 16 * (b + 1))
                if p >= 2:
                    pe.wait_ge(mt_has_lo, MP * b + p - 1)
                for c in range(CT):
                    for t in range(2 * p, min(2 * p + 2, MT)):
                        at = c * 2 * P + (t % 2) * P
                        last = nc.tensor.transpose(
                            mt_bank(p)[:, at : at + P], mem_raw[:, t, c * P : (c + 1) * P], ident[:, :])
                last.then_inc(pe_mt, 1)

            def score(b, t):
                p, m = t // 2, (t % 2) * P
                pe.wait_ge(mt_has_lo, MP * b + p + 1)
                if t >= 3:
                    pe.wait_ge(s_copied, MT * b + t - 2)
                r = rows(t)
                product(s_bank(t)[0:r, :], [
                    (mt_hi[:, p % 2, c, m : m + r], mt_lo[:, p % 2, c, m : m + r], q_hi[:, c, :], q_lo[:, c, :])
                    for c in range(CT)]).then_inc(pe_s, 1)

            def scores(b):
                pe.wait_ge(q_has_lo, CT * (b + 1))
                for p in range(MP):
                    for t in range(2 * p, min(2 * p + 2, MT)):
                        score(b, t)
                    if p + 2 < MP:
                        transpose_mem(b, p + 2)

            def transpose_max(b):
                pe.wait_ge(run_done, (MT - 1) * (b + 1))
                pe.wait_ge(s_copied, MT * (b + 1))
                for j in range(NT):
                    last = nc.tensor.transpose(
                        bank[S_BANK][:, j * P : (j + 1) * P], run[:, j * P : (j + 1) * P], ident[:, :])
                last.then_inc(pe_max_t, 1)

            def spread_max(b, first):
                pe.wait_ge(diag_done, b + 1)
                if not first:
                    pe.wait_ge(r_done, b)
                nc.tensor.matmul(bank[S_BANK + 1][:, :], ones[:, :], diag[:, :, :].rearrange("p a n -> p (a n)"),
                                 start=True, stop=True).then_inc(pe_max_rows, 1)

            def row_sums(b, behind_scores):
                pe.wait_ge(p_added, (MT - 1) * (b + 1))
                if behind_scores:
                    pe.wait_ge(s_copied, MT * (b + 1) + MT - 2)
                else:
                    pe.wait_ge(gx_done, NT * (b + 1))
                for j in range(NT):
                    last = nc.tensor.matmul(bank[S_BANK + 1][:, j : j + 1], psum_rows[:, j * P : (j + 1) * P],
                                            ones[:, 0:1], start=True, stop=True)
                last.then_inc(pe_sum, 1)

            def context(b, j, behind_scores):
                if j == 0:
                    pe.wait_ge(u_has_lo, CT * (b + 1))
                    if behind_scores:
                        pe.wait_ge(mt_has_lo, MP * (b + 2))
                        pe.wait_ge(s_copied, MT * (b + 1) + MT - 1)
                if j >= 2:
                    pe.wait_ge(ctx_copied, NT * b + j - 1)
                n = slice(j * P, (j + 1) * P)
                product(bank[CTX_BANK + j % 2][:, :], [
                    (u_hi[:, c, n], u_lo[:, c, n], wt_hi[:, c, :], wt_lo[:, c, :]) for c in range(CT)
                ]).then_inc(pe_ctx, 1)
                if j >= 2:
                    pe.wait_ge(z_done, NT * b + j - 1)
                product(bank[G_BANK + j % 2][:, :], [
                    (u_hi[:, c, n], u_lo[:, c, n], v_hi[:, c, :], v_lo[:, c, :]) for c in range(CT)
                ]).then_inc(pe_g, 1)

            def gate_x(b, j):
                if j == 0:
                    pe.wait_ge(col_max_done, b + 1)
                elif j == 1:
                    pe.wait_ge(max_copied, b + 1)
                else:
                    pe.wait_ge(gx_done, NT * b + j - 1)
                n = slice(j * P, (j + 1) * P)
                product(bank[S_BANK + j % 2][:, :], [
                    (xt_hi[:, k, n], xt_lo[:, k, n], wg1t_hi[:, k, :], wg1t_lo[:, k, :]) for k in range(DT)
                ]).then_inc(pe_gx, 1)

            def weighted(b, t):
                pe.wait_ge(p_has_lo, MT * b + t + 1)
                r = rows(t)
                for c in range(CT):
                    cs = slice(c * P, (c + 1) * P)
                    dst = bank[U_BANK + c][:, :]
                    nc.tensor.matmul(dst, mem_hi[0:r, t, cs], p_hi[0:r, t, :], start=(t == 0), stop=False)
                    nc.tensor.matmul(dst, mem_hi[0:r, t, cs], p_lo[0:r, t % LO_RING, :], start=False, stop=False)
                    last = nc.tensor.matmul(dst, mem_lo[0:r, t, cs], p_hi[0:r, t, :], start=False, stop=(t == MT - 1))
                last.then_inc(pe_u, 1)

            def weights(g):
                if g >= 8:
                    pe.wait_ge(wt_split_hi, g - 3)
                elif g >= 4:
                    pe.wait_ge(wt_split_lo, g - 3)
                dst = weight_bank(g)
                if g in V:
                    pe.wait_ge(wt_split_hi, WG2T[-1] + 1)
                    c = g - V[0]
                    for k in range(DT):
                        last = nc.tensor.matmul(dst[:, :], w_raw[:, k, c * P : (c + 1) * P], x_raw[:, k, :],
                                                start=(k == 0), stop=(k == DT - 1))
                else:
                    for i in range(DT):
                        if g in WT:
                            src = w_raw[:, i, (g - WT[0]) * P : (g - WT[0] + 1) * P]
                        else:
                            src = wg_raw[i][:, g * P : (g + 1) * P]
                        last = nc.tensor.transpose(dst[:, i * P : (i + 1) * P], src, ident[:, :])
                last.then_inc(pe_wt, 1)

            def iteration(b, first, last):
                scores(b)
                if first:
                    pe.wait_ge(in_wg, 16 * DT)
                    pe.wait_ge(mt_has_lo, MP)
                    pe.wait_ge(s_copied, MT - 1)
                    for g in WG1T:
                        weights(g)
                    transpose_max(b)
                    for g in WG2T:
                        weights(g)
                    spread_max(b, first)
                    for g in [*WT, *V]:
                        weights(g)
                    pe.wait_ge(wt_split_lo, len(WG1T))
                else:
                    row_sums(b - 1, True)
                    context(b - 1, 0, True)
                    transpose_max(b)
                    context(b - 1, 1, True)
                    spread_max(b, first)
                    context(b - 1, 2, True)
                    context(b - 1, 3, True)
                for j in range(NT):
                    gate_x(b, j)
                if not last:
                    pe.wait_ge(in_x, 16 * (b + 2))
                    if first:
                        pe.wait_ge(wt_split_lo, 8)
                    else:
                        pe.wait_ge(ctx_copied, NT * b)
                    transpose_x(b + 1, 0)
                    transpose_x(b + 1, 1)
                if not first:
                    pe.wait_ge(u_has_lo, CT * b)
                pe.wait_ge(mem_has_lo, MP * (b + 1))
                for t in range(MT):
                    weighted(b, t)
                    if t in (2, 4) and not last:
                        transpose_x(b + 1, 1 + t // 2)
                    if t == 9 and not last:
                        pe.wait_ge(xt_has_lo, DT * (b + 2))
                        pe.wait_ge(gx_done, NT * (b + 1))
                        for c in range(CT):
                            query(b + 1, c)
                        if not first:
                            pe.wait_ge(z_done, NT * b)
                        transpose_mem(b + 1, 0)
                        transpose_mem(b + 1, 1)

            pe.wait_ge(ready_ident, 1)
            pe.wait_ge(ready_ones, 1)
            pe.wait_ge(ready_pad, 1)
            pe.wait_ge(in_x, 16)
            for k in range(DT):
                transpose_x(0, k)
            pe.wait_ge(w_split_lo, 1)
            pe.wait_ge(xt_has_lo, DT)
            for c in range(CT):
                query(0, c)
            transpose_mem(0, 0)
            transpose_mem(0, 1)
            iteration(0, True, False)
            with pe.Fori(1, B - 1) as b:
                iteration(b, False, False)
            iteration(B - 1, False, True)
            row_sums(B - 1, False)
            for j in range(NT):
                context(B - 1, j, False)

        @block.scalar
        def _(act):
            def copy(dst, src):
                return nc.scalar.activation(dst, src, ACT.Copy)

            def mt_hi_part(b, p):
                act.wait_ge(pe_mt, MP * b + p + 1)
                if p >= 2:
                    act.wait_ge(pe_s, MT * b + 2 * p - 2)
                elif not (isinstance(b, int) and b == 0):
                    act.wait_ge(pe_s, MT * b)
                n = 2 * P if p < MP - 1 else P
                copy(mt_hi[:, p % 2, :, 0:n], mt_bank(p)[:, :].rearrange("p (c m) -> p c m", c=CT)[:, :, 0:n]
                     ).then_inc(mt_has_hi, 1)

            def mem_hi_part(b, p, first):
                if p == 0 and not first:
                    act.wait_ge(pe_u, MT * b)
                act.wait_ge(in_mem[p], 16 * (b + 1))
                ts = slice(2 * p, min(2 * p + 2, MT))
                copy(mem_hi[:, ts, :], mem_raw[:, ts, :]).then_inc(mem_has_hi, 1)

            def copy_s(b, t):
                act.wait_ge(pe_s, MT * b + t + 1)
                copy(s[0 : rows(t), t, :], s_bank(t)[0 : rows(t), :]).then_inc(s_copied, 1)

            def exp(b, t, first):
                act.wait_ge(shifted, MT * b + t + 1)
                if t >= TMP_RING:
                    act.wait_ge(p_has_lo, MT * b + t - TMP_RING + 1)
                    act.wait_ge(p_added, (MT - 1) * b + max(t - TMP_RING, 1))
                elif not first:
                    act.wait_ge(p_has_lo, MT * b)
                    act.wait_ge(p_added, (MT - 1) * b)
                r = rows(t)
                nc.scalar.activation(p_tmp[0:r, t % TMP_RING, :], s[0:r, t, :], ACT.Exp,
                                     scale=float(D) ** -0.5).then_inc(exp_done, 1)

            def p_hi_part(b, t):
                act.wait_ge(exp_done, MT * b + t + 1)
                r = rows(t)
                copy(p_hi[0:r, t, :], p_tmp[0:r, t % TMP_RING, :]).then_inc(p_has_hi, 1)

            def softmax(b, t, first):
                if t < MT:
                    exp(b, t, first)
                if t >= 1:
                    p_hi_part(b, t - 1)

            def copy_max(b):
                act.wait_ge(pe_max_rows, b + 1)
                if not (isinstance(b, int) and b == 0):
                    act.wait_ge(shifted, MT * b)
                copy(max_rows[:, :], bank[S_BANK + 1][:, :]).then_inc(max_copied, 1)

            def copy_ctx(b, j):
                act.wait_ge(pe_ctx, NT * b + j + 1)
                if j == 0:
                    act.wait_ge(r_done, b + 1)
                if not (isinstance(b, int) and b == 0):
                    act.wait_ge(stored[j], 16 * b)
                nc.scalar.activation(fused[:, j, :], bank[CTX_BANK + j % 2][:, :], ACT.Copy,
                                     scale=r_half[:, j : j + 1]).then_inc(ctx_copied, 1)

            def tanh(b, j):
                act.wait_ge(z_done, NT * b + j + 1)
                nc.scalar.activation(gate[:, j, :], gate[:, j, :], ACT.Tanh, scale=0.5).then_inc(tanh_done, 1)

            def squares(b, j):
                act.wait_ge(fused_done, NT * b + j + 1)
                nc.scalar.activation(gate[:, j, :], fused[:, j, :], ACT.Square,
                                     accum_out=sq_sum[:, j : j + 1]).then_inc(squares_done, 1)

            def xt_hi_part(b, k, first):
                act.wait_ge(pe_xt, DT * b + k + 1)
                if k == 0 and not first:
                    act.wait_ge(pe_gx, NT * b)
                copy(xt_hi[:, k, :], bank[CTX_BANK + k % 2][:, :]).then_inc(xt_has_hi, 1)

            def q_hi_part(b, c):
                act.wait_ge(pe_q, CT * b + c + 1)
                copy(q_hi[:, c, :], bank[S_BANK + c][:, :]).then_inc(q_has_hi, 1)

            def u_hi_part(b, c):
                act.wait_ge(pe_u, MT * (b + 1))
                copy(u_hi[:, c, :], bank[U_BANK + c][:, :]).then_inc(u_has_hi, 1)

            def weights(g):
                act.wait_ge(pe_wt, g + 1)
                if g in WG1T:
                    dst = wg1t_hi[:, g - WG1T[0], :]
                elif g in WG2T:
                    dst = x_raw[:, g - WG2T[0], :]
                elif g in WT:
                    dst = wt_hi[:, g - WT[0], :]
                else:
                    dst = v_hi[:, g - V[0], :]
                copy(dst, weight_bank(g)[:, :]).then_inc(wt_split_hi, 1)

            def iteration(b, first, last):
                for p in range(MP):
                    for t in range(2 * p, min(2 * p + 2, MT)):
                        copy_s(b, t)
                    if p + 2 < MP:
                        mt_hi_part(b, p + 2)
                    mem_hi_part(b, p, first)
                if first:
                    for g in [*WG1T, *WG2T]:
                        weights(g)
                    copy_max(b)
                    for t in range(MT + 1):
                        softmax(b, t, first)
                        if t < 4:
                            weights(WT[0] + t)
                        if not last and t in X_AT:
                            xt_hi_part(b + 1, X_AT.index(t), False)
                        if not last and t == 12:
                            q_hi_part(b + 1, 0)
                            q_hi_part(b + 1, 1)
                else:
                    copy_ctx(b - 1, 0)
                    tanh(b - 1, 0)
                    copy_ctx(b - 1, 1)
                    tanh(b - 1, 1)
                    copy_max(b)
                    for t in range(MT + 1):
                        softmax(b, t, first)
                        if t == 1:
                            copy_ctx(b - 1, 2)
                        if t == 2:
                            tanh(b - 1, 2)
                            copy_ctx(b - 1, 3)
                        if t == 3:
                            tanh(b - 1, 3)
                            squares(b - 1, 0)
                            squares(b - 1, 1)
                        if t == 4:
                            squares(b - 1, 2)
                            squares(b - 1, 3)
                        if not last and t in X_AT:
                            xt_hi_part(b + 1, X_AT.index(t), False)
                        if not last and t == 13:
                            q_hi_part(b + 1, 0)
                            q_hi_part(b + 1, 1)
                if not last:
                    mt_hi_part(b + 1, 0)
                    mt_hi_part(b + 1, 1)
                for c in range(CT):
                    u_hi_part(b, c)

            act.wait_ge(in_w, 16)
            copy(w_hi[:, :, :], w_raw).then_inc(w_split_hi, 1)
            for k in range(DT):
                xt_hi_part(0, k, True)
            for c in range(CT):
                q_hi_part(0, c)
            act.wait_ge(ready_pad, 1)
            mt_hi_part(0, 0)
            mt_hi_part(0, 1)
            iteration(0, True, False)
            with act.Fori(1, B - 1) as b:
                iteration(b, False, False)
            iteration(B - 1, False, True)
            for j in range(NT):
                copy_ctx(B - 1, j)
                tanh(B - 1, j)
                if j >= 1:
                    squares(B - 1, j - 1)
            squares(B - 1, NT - 1)

        @block.vector
        def _(dve):
            def lo_part(dst, src, hi):
                return nc.vector.tensor_tensor(dst, src, hi.bitcast(F32), ALU.subtract)

            def running_max(b, t):
                dve.wait_ge(s_copied, MT * b + t + 1)
                r = rows(t)
                if t == 1:
                    a = s[0:r, 0, :]
                else:
                    a = run[0:r, :]
                    dve.wait_ge(run_done, (MT - 1) * b + t - 1)
                nc.vector.tensor_tensor(run[0:r, :], a, s[0:r, t, :], ALU.max).then_inc(run_done, 1)

            def mt_lo_part(b, p):
                dve.wait_ge(mt_has_hi, MP * b + p + 1)
                n = 2 * P if p < MP - 1 else P
                lo_part(mt_lo[:, p % 2, :, 0:n], mt_bank(p)[:, :].rearrange("p (c m) -> p c m", c=CT)[:, :, 0:n],
                        mt_hi[:, p % 2, :, 0:n]).then_inc(mt_has_lo, 1)

            def mem_lo_part(b, p):
                dve.wait_ge(mem_has_hi, MP * b + p + 1)
                ts = slice(2 * p, min(2 * p + 2, MT))
                lo_part(mem_lo[:, ts, :], mem_raw[:, ts, :], mem_hi[:, ts, :]).then_inc(mem_has_lo, 1)

            def reduce_max(b):
                dve.wait_ge(pe_max_t, b + 1)
                nc.vector.tensor_reduce(col_max[:, :], bank[S_BANK][:, :].rearrange("p (a n) -> p a n", a=NT),
                                        AX.X, ALU.max).then_inc(col_max_done, 1)
                dve.wait_ge(col_max_done, b + 1)
                nc.vector.tensor_tensor(diag[:, :, :], ident[:, :].unsqueeze(1).broadcast_to([P, NT, P]),
                                        col_max[:, :].unsqueeze(2).broadcast_to([P, NT, P]),
                                        ALU.mult).then_inc(diag_done, 1)

            def shift(b, t):
                if t == 0:
                    dve.wait_ge(max_copied, b + 1)
                r = rows(t)
                nc.vector.tensor_tensor(s[0:r, t, :], s[0:r, t, :], max_rows[0:r, :],
                                        ALU.subtract).then_inc(shifted, 1)

            def p_lo_part(b, t):
                dve.wait_ge(p_has_hi, MT * b + t + 1)
                if t >= LO_RING:
                    dve.wait_ge(pe_u, MT * b + t - LO_RING + 1)
                r = rows(t)
                lo_part(p_lo[0:r, t % LO_RING, :], p_tmp[0:r, t % TMP_RING, :], p_hi[0:r, t, :]).then_inc(p_has_lo, 1)

            def softmax(b, t):
                if t + 2 < MT:
                    shift(b, t + 2)
                p_lo_part(b, t)

            def add_bias(b, j, first):
                dve.wait_ge(pe_gx, NT * b + j + 1)
                if j == 0 and not first:
                    dve.wait_ge(squares_done, NT * b)
                nc.vector.tensor_tensor(gate[:, j, :], bank[S_BANK + j % 2][:, :], bias_rows[:, :],
                                        ALU.add).then_inc(gx_done, 1)

            def xt_lo_part(b, k):
                dve.wait_ge(xt_has_hi, DT * b + k + 1)
                lo_part(xt_lo[:, k, :], bank[CTX_BANK + k % 2][:, :], xt_hi[:, k, :]).then_inc(xt_has_lo, 1)

            def q_lo_part(b, c):
                dve.wait_ge(q_has_hi, CT * b + c + 1)
                lo_part(q_lo[:, c, :], bank[S_BANK + c][:, :], q_hi[:, c, :]).then_inc(q_has_lo, 1)

            def u_lo_part(b, c):
                dve.wait_ge(u_has_hi, CT * b + c + 1)
                lo_part(u_lo[:, c, :], bank[U_BANK + c][:, :], u_hi[:, c, :]).then_inc(u_has_lo, 1)

            def reciprocal(b):
                dve.wait_ge(pe_sum, b + 1)
                nc.vector.reciprocal(r_sum[:, :], bank[S_BANK + 1][:, 0:NT]).then_inc(r_first, 1)
                dve.wait_ge(r_first, b + 1)
                nc.vector.tensor_scalar(r_half[:, :], r_sum[:, :], 0.5, None, ALU.mult).then_inc(r_done, 1)

            def gate_input(b, j):
                dve.wait_ge(pe_g, NT * b + j + 1)
                nc.vector.scalar_tensor_tensor(gate[:, j, :], bank[G_BANK + j % 2][:, :], r_sum[:, j : j + 1],
                                               gate[:, j, :], ALU.mult, ALU.add).then_inc(z_done, 1)

            def fuse(b, j):
                dve.wait_ge(tanh_done, NT * b + j + 1)
                dve.wait_ge(ctx_copied, NT * b + j + 1)
                nc.vector.scalar_tensor_tensor(fused[:, j, :], gate[:, j, :], 1.0, fused[:, j, :],
                                               ALU.add, ALU.mult).then_inc(gated, 1)
                dve.wait_ge(gated, NT * b + j + 1)
                dve.wait_ge(in_x_again[j % 2], 16 * (2 * b + j // 2 + 1))
                nc.vector.tensor_tensor(fused[:, j, :], fused[:, j, :], x_again[:, j % 2, :],
                                        ALU.add).then_inc(fused_done, 1)

            def rms(b):
                count = [NEWTON_OPS * b]

                def link(instruction):
                    count[0] = count[0] + 1
                    instruction.then_inc(newton, 1)
                    dve.wait_ge(newton, count[0])

                dve.wait_ge(squares_done, NT * (b + 1))
                link(nc.vector.tensor_scalar(mean_sq[:, :], sq_sum[:, :], 1.0 / D, EPS, ALU.mult, ALU.add))
                link(nc.vector.tensor_scalar(r_rms[:, :].bitcast(I32), mean_sq[:, :].bitcast(I32), -0.5, RSQRT_MAGIC,
                                             ALU.mult, ALU.add))
                for _ in range(NEWTON_STEPS):
                    link(nc.vector.tensor_tensor(nw_a[:, :], r_rms[:, :], mean_sq[:, :], ALU.mult))
                    link(nc.vector.scalar_tensor_tensor(nw_b[:, :], nw_a[:, :], -0.5, r_rms[:, :], ALU.mult, ALU.mult))
                    link(nc.vector.scalar_tensor_tensor(r_rms[:, :], nw_b[:, :], 1.5, r_rms[:, :], ALU.add, ALU.mult))

            def output(b, j):
                nc.vector.scalar_tensor_tensor(fused[:, j, :], fused[:, j, :], r_rms[:, j : j + 1], norm_rows[:, :],
                                               ALU.mult, ALU.mult).then_inc(out_done, 1)

            def weights(g, n):
                dve.wait_ge(wt_split_hi, g + 1)
                if g in WG1T:
                    hi, lo = wg1t_hi[:, g - WG1T[0], :], wg1t_lo[:, g - WG1T[0], :]
                elif g in WT:
                    hi, lo = wt_hi[:, g - WT[0], :], wt_lo[:, g - WT[0], :]
                else:
                    hi, lo = v_hi[:, g - V[0], :], v_lo[:, g - V[0], :]
                lo_part(lo, weight_bank(g)[:, :], hi).then_inc(wt_split_lo, 1)

            def iteration(b, first, last):
                for p in range(MP):
                    for t in range(2 * p, min(2 * p + 2, MT)):
                        if t >= 1:
                            running_max(b, t)
                    if p + 2 < MP:
                        mt_lo_part(b, p + 2)
                    mem_lo_part(b, p)
                if first:
                    dve.wait_ge(in_rows, 32)
                    for g in WG1T:
                        weights(g, g)
                    reduce_max(b)
                    shift(b, 0)
                    shift(b, 1)
                    for t in range(MT):
                        softmax(b, t)
                        if t < 4:
                            weights(WT[0] + t, 0)
                        if 2 <= t < 2 + NT:
                            add_bias(b, t - 2, first)
                        if t in X_AT:
                            xt_lo_part(b + 1, X_AT.index(t))
                else:
                    reciprocal(b - 1)
                    gate_input(b - 1, 0)
                    reduce_max(b)
                    gate_input(b - 1, 1)
                    fuse(b - 1, 0)
                    shift(b, 0)
                    shift(b, 1)
                    fuse(b - 1, 1)
                    for t in range(MT):
                        softmax(b, t)
                        if t == 0:
                            gate_input(b - 1, 2)
                        if t == 1:
                            gate_input(b - 1, 3)
                            fuse(b - 1, 2)
                        if t == 2:
                            fuse(b - 1, 3)
                        if t == 4:
                            rms(b - 1)
                        if 3 <= t < 3 + NT:
                            add_bias(b, t - 3, first)
                        if 5 <= t < 5 + NT:
                            output(b - 1, t - 5)
                        if not last and t in X_AT:
                            xt_lo_part(b + 1, X_AT.index(t))
                if not last:
                    q_lo_part(b + 1, 0)
                    q_lo_part(b + 1, 1)
                    mt_lo_part(b + 1, 0)
                    mt_lo_part(b + 1, 1)
                for c in range(CT):
                    u_lo_part(b, c)

            nc.vector.memset(ones[:, :], 1.0).then_inc(ready_ones, 1)
            nc.vector.memset(mem_raw[:, MT - 1, :], 0.0).then_inc(ready_pad, 1)
            dve.wait_ge(w_split_hi, 1)
            lo_part(w_lo[:, :, :], w_raw, w_hi[:, :, :]).then_inc(w_split_lo, 1)
            for k in range(DT):
                xt_lo_part(0, k)
            for c in range(CT):
                q_lo_part(0, c)
            mt_lo_part(0, 0)
            mt_lo_part(0, 1)
            iteration(0, True, False)
            with dve.Fori(1, B - 1) as b:
                iteration(b, False, False)
            iteration(B - 1, False, True)
            reciprocal(B - 1)
            for j in range(NT):
                gate_input(B - 1, j)
                if j >= 1:
                    fuse(B - 1, j - 1)
            fuse(B - 1, NT - 1)
            rms(B - 1)
            for j in range(NT):
                output(B - 1, j)

        @block.gpsimd
        def _(pool):
            def add_p(b, t, first):
                pool.wait_ge(exp_done, MT * b + t + 1)
                r = rows(t)
                if t == 1:
                    if not first:
                        pool.wait_ge(pe_sum, b)
                    a = p_tmp[0:r, 0, :]
                else:
                    pool.wait_ge(p_added, (MT - 1) * b + t - 1)
                    a = psum_rows[0:r, :]
                nc.gpsimd.tensor_tensor(psum_rows[0:r, :], a, p_tmp[0:r, t % TMP_RING, :], ALU.add).then_inc(p_added, 1)

            nc.gpsimd.memset(ident[:, :], 0.0).then_inc(cleared, 1)
            pool.wait_ge(cleared, 1)
            nc.gpsimd.affine_select(out=ident[:, :], in_=ident[:, :], compare_op=ALU.not_equal, fill=1.0, base=0,
                                    pattern=[[-1, P]], channel_multiplier=1).then_inc(ready_ident, 1)
            for t in range(1, MT):
                add_p(0, t, True)
            with pool.Fori(1, B) as b:
                for t in range(1, MT):
                    add_p(b, t, False)


_INS = ["x", "ctx_1024", "L0_xattn_W_mem", "L0_xattn_W_gate", "L0_xattn_b_gate", "L0_xattn_norm_w"]
_OUTS = [((8, 512, 512), "float32")]


def kernel(**inputs):
    import numpy as _np
    import concourse.bacc as _bacc
    from concourse import mybir as _mybir
    from concourse.bass_utils import run_bass_kernel_spmd as _run

    nc = _bacc.Bacc("TRN2", target_bir_lowering=False, num_devices=1)
    arrays, args = {}, []
    for name in _INS:
        a = _np.ascontiguousarray(inputs[name])
        arrays[f"in_{name}_dram"] = a
        args.append(nc.dram_tensor(f"in_{name}_dram", a.shape, _mybir.dt.from_np(a.dtype), kind="ExternalInput").ap())
    for i, (shape, dtype) in enumerate(_OUTS):
        dt = _mybir.dt.from_np(_np.dtype(dtype))
        args.append(nc.dram_tensor(f"out_{i}_dram", shape, dt, kind="ExternalOutput").ap())
    xattn_kernel(nc, *args)
    r = _run(nc, [arrays], core_ids=[0])
    return r.results[0]["out_0_dram"]
```

```python
from contextlib import ExitStack

import concourse.bass as bass
from concourse import mybir

ALU = mybir.AluOpType
ACT = mybir.ActivationFunctionType
AX = mybir.AxisListType
F32 = mybir.dt.float32
F32R = mybir.dt.float32r
I32 = mybir.dt.int32

P = 128
EPS = 1e-6
RSQRT_MAGIC = float(0x5F3759DF)
NEWTON_STEPS = 3


def xattn_kernel(nc: bass.Bass, x, mem, w, wg, b_gate, norm_w, out):
    B, N, D = x.shape
    _, M, C = mem.shape
    NT = N // P
    DT = D // P
    CT = C // P
    MT = -(-M // P)
    LAST = M - (MT - 1) * P
    MP = -(-MT // 2)
    TMP_RING = 4
    LO_RING = 10
    assert N == 512 and D == 512 and C == 256 and MT % 2 == 1

    def rows(t):
        return P if t < MT - 1 else LAST

    with ExitStack() as ctx:

        def sb(name, shape, dt=F32):
            return ctx.enter_context(nc.sbuf_tensor(name, shape, dt))

        def sem(name):
            return ctx.enter_context(nc.semaphore(name))

        s_offset = -(-nc.sbuf_base // 32) * 32
        s = sb("s", [P, MT, N])
        p_hi = nc.alloc_sbuf_tensor_at("p_hi", [P, MT, N], F32R, offset=s_offset)
        p_tmp = sb("p_tmp", [P, TMP_RING, N])
        p_lo = sb("p_lo", [P, LO_RING, N], F32R)
        mem_raw = sb("mem_raw", [P, MT, C])
        mem_hi = sb("mem_hi", [P, MT, C], F32R)
        mem_lo = sb("mem_lo", [P, MT, C], F32R)
        mt_hi = sb("mt_hi", [P, 2, CT, 2 * P], F32R)
        mt_lo = sb("mt_lo", [P, 2, CT, 2 * P], F32R)
        x_raw = sb("x_raw", [P, NT, D])
        xt_hi = sb("xt_hi", [P, DT, N], F32R)
        xt_lo = sb("xt_lo", [P, DT, N], F32R)
        q_hi = sb("q_hi", [P, CT, N], F32R)
        q_lo = sb("q_lo", [P, CT, N], F32R)
        u_hi = sb("u_hi", [P, CT, N], F32R)
        u_lo = sb("u_lo", [P, CT, N], F32R)
        gate = sb("gate", [P, NT, D])
        fused = sb("fused", [P, NT, D])
        squares_out = sb("squares_out", [P, D])
        x_again = sb("x_again", [P, 2, D])
        w_hi = sb("w_hi", [P, DT, C], F32R)
        w_lo = sb("w_lo", [P, DT, C], F32R)
        wt_hi = sb("wt_hi", [P, CT, D], F32R)
        wt_lo = sb("wt_lo", [P, CT, D], F32R)
        wg1t_hi = sb("wg1t_hi", [P, DT, D], F32R)
        wg1t_lo = sb("wg1t_lo", [P, DT, D], F32R)
        v_hi = sb("v_hi", [P, CT, D], F32R)
        v_lo = sb("v_lo", [P, CT, D], F32R)
        bias_rows = sb("bias_rows", [P, D])
        norm_rows = sb("norm_rows", [P, D])
        run = sb("run", [P, N])
        max_rows = sb("max_rows", [P, N])
        psum_rows = sb("psum_rows", [P, N])
        diag = sb("diag", [P, NT, P])
        ident = sb("ident", [P, P])
        ones = sb("ones", [P, P])
        col_max = sb("col_max", [P, NT])
        r_sum = sb("r_sum", [P, NT])
        r_half = sb("r_half", [P, NT])
        sq_sum = sb("sq_sum", [P, NT])
        mean_sq = sb("mean_sq", [P, NT])
        r_rms = sb("r_rms", [P, NT])
        nw_a = sb("nw_a", [P, NT])
        nw_b = sb("nw_b", [P, NT])
        w_raw = x_again[:, :, :].rearrange("p a (k c) -> p (a k) c", c=C)
        wg_raw = [
            (gate, fused)[i // 2][:, 2 * (i % 2) : 2 * (i % 2) + 2, :].rearrange("p a f -> p (a f)")
            for i in range(DT)
        ]

        bank = [ctx.enter_context(nc.psum_tensor(f"bank{i}", [P, 512], F32)) for i in range(8)]
        U_BANK, S_BANK, G_BANK, CTX_BANK = 0, 2, 4, 6

        def x_bank(k, first):
            return bank[(6, 7, 4, 0)[k] if first else CTX_BANK + k % 2]

        def s_bank(t):
            return bank[S_BANK + t % 3]

        def mt_bank(p):
            return bank[5 + p % 2]

        in_x, in_w, in_wg, in_rows = sem("in_x"), sem("in_w"), sem("in_wg"), sem("in_rows")
        in_x_first = [sem(f"in_x_first{k}") for k in range(DT)]
        in_mem = [sem(f"in_mem{p}") for p in range(MP)]
        in_x_again = [sem(f"in_x_again{i}") for i in range(2)]
        stored = [sem(f"stored{j}") for j in range(NT)]
        cleared, ready_ident, ready_ones, ready_pad = (
            sem("cleared"), sem("ready_ident"), sem("ready_ones"), sem("ready_pad"))
        w_split_hi, w_split_lo = sem("w_split_hi"), sem("w_split_lo")
        pe_wt, wt_split_hi, wt_split_lo = sem("pe_wt"), sem("wt_split_hi"), sem("wt_split_lo")
        pe_mt, pe_s, pe_max_t, pe_max_rows = sem("pe_mt"), sem("pe_s"), sem("pe_max_t"), sem("pe_max_rows")
        pe_sum, pe_ctx, pe_g, pe_gx = sem("pe_sum"), sem("pe_ctx"), sem("pe_g"), sem("pe_gx")
        pe_xt, pe_q, pe_u = sem("pe_xt"), sem("pe_q"), sem("pe_u")
        s_copied, mt_has_hi, mem_has_hi = sem("s_copied"), sem("mt_has_hi"), sem("mem_has_hi")
        exp_done, p_has_hi, xt_has_hi = sem("exp_done"), sem("p_has_hi"), sem("xt_has_hi")
        q_has_hi, u_has_hi, max_copied = sem("q_has_hi"), sem("u_has_hi"), sem("max_copied")
        ctx_copied, tanh_done, squares_done = sem("ctx_copied"), sem("tanh_done"), sem("squares_done")
        run_done, mt_has_lo, mem_has_lo = sem("run_done"), sem("mt_has_lo"), sem("mem_has_lo")
        col_max_done, diag_done, shifted = sem("col_max_done"), sem("diag_done"), sem("shifted")
        p_has_lo, xt_has_lo, q_has_lo = sem("p_has_lo"), sem("xt_has_lo"), sem("q_has_lo")
        u_has_lo, gx_done, r_first, r_done = sem("u_has_lo"), sem("gx_done"), sem("r_first"), sem("r_done")
        z_done, gated, fused_done = sem("z_done"), sem("gated"), sem("fused_done")
        newton, out_done = sem("newton"), sem("out_done")
        p_added = sem("p_added")

        NEWTON_OPS = 2 + 3 * NEWTON_STEPS
        WG1T, WG2T, V, WT = range(0, 4), range(4, 8), range(8, 10), range(10, 12)

        X_AT = [7, 8, 10, 11]

        def weight_bank(g):
            return bank[4 + g % 4]

        block = ctx.enter_context(nc.Block())

        @block.sync
        def _(sp):
            def load_x(b):
                sp.dma_start(x_raw[:, :, :], x[b].rearrange("(t p) d -> p t d", p=P)).then_inc(in_x, 16)

            def load_mem(b, p):
                if p < MP - 1:
                    src = mem[b, 2 * p * P : (2 * p + 2) * P, :].rearrange("(t p) c -> p t c", p=P)
                    sp.dma_start(mem_raw[:, 2 * p : 2 * p + 2, :], src).then_inc(in_mem[p], 16)
                else:
                    sp.dma_start(mem_raw[0:LAST, MT - 1, :], mem[b, (MT - 1) * P : M, :]).then_inc(in_mem[p], 16)

            def load_x_again(b, j):
                sp.dma_start(x_again[:, j % 2, :], x[b, j * P : (j + 1) * P, :]).then_inc(in_x_again[j % 2], 16)

            def store(b, j):
                sp.wait_ge(out_done, NT * b + j + 1)
                sp.dma_start(out[b, j * P : (j + 1) * P, :], fused[:, j, :]).then_inc(stored[j], 16)

            def finish_io(b):
                for j in range(2, NT):
                    sp.wait_ge(fused_done, NT * b + j - 1)
                    load_x_again(b, j)
                for j in range(NT):
                    store(b, j)

            def iteration(b, first, last):
                if not last:
                    sp.wait_ge(pe_xt, DT * (b + 1))
                    if first:
                        sp.wait_ge(pe_wt, V[-1] + 1)
                    load_x(b + 1)
                if not first:
                    sp.wait_ge(fused_done, NT * (b - 1))
                    load_x_again(b - 1, 0)
                    load_x_again(b - 1, 1)
                if not last:
                    for p in range(MP):
                        sp.wait_ge(pe_mt, MP * b + p + 1)
                        sp.wait_ge(mem_has_lo, MP * b + p + 1)
                        load_mem(b + 1, p)
                if not first:
                    finish_io(b - 1)

            for k in range(DT):
                src = x[0, :, k * P : (k + 1) * P].rearrange("(t p) d -> p t d", p=P)
                sp.dma_start(x_raw[:, :, k * P : (k + 1) * P], src).then_inc(in_x_first[k], 16)
            load_mem(0, 2)
            for i in range(DT):
                sp.dma_start(wg_raw[i], wg[i * P : (i + 1) * P, :]).then_inc(in_wg, 16)
            sp.wait_ge(ready_pad, 1)
            for p in range(3, MP):
                load_mem(0, p)
            sp.dma_start(bias_rows[:, :], b_gate.partition_broadcast(P)).then_inc(in_rows, 16)
            sp.dma_start(norm_rows[:, :], norm_w.partition_broadcast(P)).then_inc(in_rows, 16)

            for p in range(MP):
                sp.wait_ge(pe_mt, p + 1)
                sp.wait_ge(mem_has_lo, p + 1)
                load_mem(1, p)
            sp.wait_ge(pe_wt, V[-1] + 1)
            load_x(1)
            with sp.Fori(1, B - 1) as b:
                iteration(b, False, False)
            iteration(B - 1, False, True)
            sp.wait_ge(fused_done, NT * (B - 1))
            load_x_again(B - 1, 0)
            load_x_again(B - 1, 1)
            finish_io(B - 1)
            for j in range(NT):
                sp.wait_ge(stored[j], 16 * B)

        @block.tensor
        def _(pe):
            def product(dst, terms, start=True, stop=True):
                n = len(terms)
                for i, (a_hi, a_lo, b_hi, b_lo) in enumerate(terms):
                    nc.tensor.matmul(dst, a_hi, b_hi, start=(start and i == 0), stop=False)
                    nc.tensor.matmul(dst, a_hi, b_lo, start=False, stop=False)
                    last = nc.tensor.matmul(dst, a_lo, b_hi, start=False, stop=(stop and i == n - 1))
                return last

            def transpose_x(b, k, first=False):
                if first:
                    pe.wait_ge(in_x_first[k], 16)
                elif k >= 2:
                    pe.wait_ge(xt_has_lo, DT * b + k - 1)
                for j in range(NT):
                    last = nc.tensor.transpose(
                        x_bank(k, first)[:, j * P : (j + 1) * P], x_raw[:, j, k * P : (k + 1) * P], ident[:, :])
                last.then_inc(pe_xt, 1)

            def query(c, ks):
                last = product(bank[S_BANK + c][:, :], [
                    (w_hi[:, k, c * P : (c + 1) * P], w_lo[:, k, c * P : (c + 1) * P], xt_hi[:, k, :], xt_lo[:, k, :])
                    for k in ks], start=(ks[0] == 0), stop=(ks[-1] == DT - 1))
                if ks[-1] == DT - 1:
                    last.then_inc(pe_q, 1)

            def transpose_mem(b, p):
                pe.wait_ge(in_mem[p], 16 * (b + 1))
                if p >= 2:
                    pe.wait_ge(mt_has_lo, MP * b + p - 1)
                for c in range(CT):
                    for t in range(2 * p, min(2 * p + 2, MT)):
                        at = c * 2 * P + (t % 2) * P
                        last = nc.tensor.transpose(
                            mt_bank(p)[:, at : at + P], mem_raw[:, t, c * P : (c + 1) * P], ident[:, :])
                last.then_inc(pe_mt, 1)

            def score(b, t):
                p, m = t // 2, (t % 2) * P
                pe.wait_ge(mt_has_lo, MP * b + p + 1)
                if t >= 3:
                    pe.wait_ge(s_copied, MT * b + t - 2)
                r = rows(t)
                product(s_bank(t)[0:r, :], [
                    (mt_hi[:, p % 2, c, m : m + r], mt_lo[:, p % 2, c, m : m + r], q_hi[:, c, :], q_lo[:, c, :])
                    for c in range(CT)]).then_inc(pe_s, 1)

            def scores(b):
                pe.wait_ge(q_has_lo, CT * (b + 1))
                for p in range(MP):
                    for t in range(2 * p, min(2 * p + 2, MT)):
                        score(b, t)
                    if p + 2 < MP:
                        transpose_mem(b, p + 2)

            def transpose_max(b):
                pe.wait_ge(run_done, (MT - 1) * (b + 1))
                pe.wait_ge(s_copied, MT * (b + 1))
                for j in range(NT):
                    last = nc.tensor.transpose(
                        bank[S_BANK][:, j * P : (j + 1) * P], run[:, j * P : (j + 1) * P], ident[:, :])
                last.then_inc(pe_max_t, 1)

            def spread_max(b, first):
                pe.wait_ge(diag_done, b + 1)
                if not first:
                    pe.wait_ge(r_done, b)
                nc.tensor.matmul(bank[S_BANK + 1][:, :], ones[:, :], diag[:, :, :].rearrange("p a n -> p (a n)"),
                                 start=True, stop=True).then_inc(pe_max_rows, 1)

            def row_sums(b, behind_scores):
                pe.wait_ge(p_added, (MT - 1) * (b + 1))
                if behind_scores:
                    pe.wait_ge(s_copied, MT * (b + 1) + MT - 2)
                else:
                    pe.wait_ge(gx_done, NT * (b + 1))
                for j in range(NT):
                    last = nc.tensor.matmul(bank[S_BANK + 1][:, j : j + 1], psum_rows[:, j * P : (j + 1) * P],
                                            ones[:, 0:1], start=True, stop=True)
                last.then_inc(pe_sum, 1)

            def gate_context(b, j, behind_scores):
                if j == 0:
                    pe.wait_ge(u_has_lo, CT * (b + 1))
                    if behind_scores:
                        pe.wait_ge(mt_has_lo, MP * (b + 2))
                        pe.wait_ge(s_copied, MT * (b + 1) + MT - 1)
                if j >= 2:
                    pe.wait_ge(z_done, NT * b + j - 1)
                n = slice(j * P, (j + 1) * P)
                product(bank[G_BANK + j % 2][:, :], [
                    (u_hi[:, c, n], u_lo[:, c, n], v_hi[:, c, :], v_lo[:, c, :]) for c in range(CT)
                ]).then_inc(pe_g, 1)

            def context(b, j):
                if j >= 2:
                    pe.wait_ge(ctx_copied, NT * b + j - 1)
                n = slice(j * P, (j + 1) * P)
                product(bank[CTX_BANK + j % 2][:, :], [
                    (u_hi[:, c, n], u_lo[:, c, n], wt_hi[:, c, :], wt_lo[:, c, :]) for c in range(CT)
                ]).then_inc(pe_ctx, 1)

            def gate_x(b, j):
                if j == 0:
                    pe.wait_ge(col_max_done, b + 1)
                elif j == 1:
                    pe.wait_ge(max_copied, b + 1)
                else:
                    pe.wait_ge(gx_done, NT * b + j - 1)
                n = slice(j * P, (j + 1) * P)
                product(bank[S_BANK + j % 2][:, :], [
                    (xt_hi[:, k, n], xt_lo[:, k, n], wg1t_hi[:, k, :], wg1t_lo[:, k, :]) for k in range(DT)
                ]).then_inc(pe_gx, 1)

            def weighted(b, t):
                pe.wait_ge(p_has_lo, MT * b + t + 1)
                r = rows(t)
                for c in range(CT):
                    cs = slice(c * P, (c + 1) * P)
                    dst = bank[U_BANK + c][:, :]
                    nc.tensor.matmul(dst, mem_hi[0:r, t, cs], p_hi[0:r, t, :], start=(t == 0), stop=False)
                    nc.tensor.matmul(dst, mem_hi[0:r, t, cs], p_lo[0:r, t % LO_RING, :], start=False, stop=False)
                    last = nc.tensor.matmul(dst, mem_lo[0:r, t, cs], p_hi[0:r, t, :], start=False, stop=(t == MT - 1))
                last.then_inc(pe_u, 1)

            def weights(g):
                if g >= 8:
                    pe.wait_ge(wt_split_hi, g - 3)
                elif g >= 4:
                    pe.wait_ge(wt_split_lo, g - 3)
                dst = weight_bank(g)
                if g in V:
                    pe.wait_ge(wt_split_hi, WG2T[-1] + 1)
                    c = g - V[0]
                    for k in range(DT):
                        last = nc.tensor.matmul(dst[:, :], w_raw[:, k, c * P : (c + 1) * P], x_raw[:, k, :],
                                                start=(k == 0), stop=(k == DT - 1))
                else:
                    for i in range(DT):
                        if g in WT:
                            src = w_raw[:, i, (g - WT[0]) * P : (g - WT[0] + 1) * P]
                        else:
                            src = wg_raw[i][:, g * P : (g + 1) * P]
                        last = nc.tensor.transpose(dst[:, i * P : (i + 1) * P], src, ident[:, :])
                last.then_inc(pe_wt, 1)

            def iteration(b, first, last):
                scores(b)
                if first:
                    pe.wait_ge(in_wg, 16 * DT)
                    pe.wait_ge(mt_has_lo, MP)
                    pe.wait_ge(s_copied, MT - 1)
                    for g in WG1T:
                        weights(g)
                    transpose_max(b)
                    for g in WG2T:
                        weights(g)
                    weights(V[0])
                    spread_max(b, first)
                    for g in [V[1], *WT]:
                        weights(g)
                    pe.wait_ge(wt_split_lo, len(WG1T))
                else:
                    row_sums(b - 1, True)
                    gate_context(b - 1, 0, True)
                    transpose_max(b)
                    context(b - 1, 0)
                    gate_context(b - 1, 1, True)
                    spread_max(b, first)
                    context(b - 1, 1)
                    for j in (2, 3):
                        gate_context(b - 1, j, True)
                        context(b - 1, j)
                for j in range(NT):
                    gate_x(b, j)
                if not last:
                    pe.wait_ge(in_x, 16 * (b + 1))
                    if first:
                        pe.wait_ge(wt_split_lo, 8)
                    else:
                        pe.wait_ge(ctx_copied, NT * b)
                    transpose_x(b + 1, 0)
                    transpose_x(b + 1, 1)
                if not first:
                    pe.wait_ge(u_has_lo, CT * b)
                pe.wait_ge(mem_has_lo, MP * (b + 1))
                for t in range(MT):
                    weighted(b, t)
                    if t in (3, 5) and not last:
                        transpose_x(b + 1, 2 if t == 3 else 3)
                    if t == 9 and not last:
                        pe.wait_ge(xt_has_lo, DT * (b + 2))
                        pe.wait_ge(gx_done, NT * (b + 1))
                        for c in range(CT):
                            query(c, range(DT))
                        if not first:
                            pe.wait_ge(z_done, NT * b)
                        transpose_mem(b + 1, 0)
                        transpose_mem(b + 1, 1)

            pe.wait_ge(ready_ident, 1)
            pe.wait_ge(ready_ones, 1)
            pe.wait_ge(ready_pad, 1)
            for k in range(DT):
                transpose_x(0, k, True)
            transpose_mem(0, 0)
            pe.wait_ge(w_split_lo, 1)
            for k in range(DT):
                pe.wait_ge(xt_has_lo, k + 1)
                for c in range(CT):
                    query(c, [k])
            transpose_mem(0, 1)
            iteration(0, True, False)
            with pe.Fori(1, B - 1) as b:
                iteration(b, False, False)
            iteration(B - 1, False, True)
            row_sums(B - 1, False)
            for j in range(NT):
                gate_context(B - 1, j, False)
                context(B - 1, j)

        @block.scalar
        def _(act):
            def copy(dst, src):
                return nc.scalar.activation(dst, src, ACT.Copy)

            def mt_hi_part(b, p):
                act.wait_ge(pe_mt, MP * b + p + 1)
                if p >= 2:
                    act.wait_ge(pe_s, MT * b + 2 * p - 2)
                elif not (isinstance(b, int) and b == 0):
                    act.wait_ge(pe_s, MT * b)
                n = 2 * P if p < MP - 1 else P
                copy(mt_hi[:, p % 2, :, 0:n], mt_bank(p)[:, :].rearrange("p (c m) -> p c m", c=CT)[:, :, 0:n]
                     ).then_inc(mt_has_hi, 1)

            def mem_hi_part(b, p, first):
                if p == 0 and not first:
                    act.wait_ge(pe_u, MT * b)
                act.wait_ge(in_mem[p], 16 * (b + 1))
                ts = slice(2 * p, min(2 * p + 2, MT))
                copy(mem_hi[:, ts, :], mem_raw[:, ts, :]).then_inc(mem_has_hi, 1)

            def copy_s(b, t):
                act.wait_ge(pe_s, MT * b + t + 1)
                copy(s[0 : rows(t), t, :], s_bank(t)[0 : rows(t), :]).then_inc(s_copied, 1)

            def exp(b, t, first):
                act.wait_ge(shifted, MT * b + t + 1)
                if t >= TMP_RING:
                    act.wait_ge(p_has_lo, MT * b + t - TMP_RING + 1)
                    act.wait_ge(p_added, (MT - 1) * b + max(t - TMP_RING, 1))
                elif not first:
                    act.wait_ge(p_has_lo, MT * b)
                    act.wait_ge(p_added, (MT - 1) * b)
                r = rows(t)
                nc.scalar.activation(p_tmp[0:r, t % TMP_RING, :], s[0:r, t, :], ACT.Exp,
                                     scale=float(D) ** -0.5).then_inc(exp_done, 1)

            def p_hi_part(b, t):
                act.wait_ge(exp_done, MT * b + t + 1)
                r = rows(t)
                copy(p_hi[0:r, t, :], p_tmp[0:r, t % TMP_RING, :]).then_inc(p_has_hi, 1)

            def softmax(b, t, first):
                if t < MT:
                    exp(b, t, first)
                if t >= 1:
                    p_hi_part(b, t - 1)

            def copy_max(b):
                act.wait_ge(pe_max_rows, b + 1)
                if not (isinstance(b, int) and b == 0):
                    act.wait_ge(shifted, MT * b)
                copy(max_rows[:, :], bank[S_BANK + 1][:, :]).then_inc(max_copied, 1)

            def copy_ctx(b, j):
                act.wait_ge(pe_ctx, NT * b + j + 1)
                if j == 0:
                    act.wait_ge(r_done, b + 1)
                if not (isinstance(b, int) and b == 0):
                    act.wait_ge(stored[j], 16 * b)
                nc.scalar.activation(fused[:, j, :], bank[CTX_BANK + j % 2][:, :], ACT.Copy,
                                     scale=r_half[:, j : j + 1]).then_inc(ctx_copied, 1)

            def tanh(b, j):
                act.wait_ge(z_done, NT * b + j + 1)
                nc.scalar.activation(gate[:, j, :], gate[:, j, :], ACT.Tanh, scale=0.5).then_inc(tanh_done, 1)

            def squares(b, j):
                act.wait_ge(fused_done, NT * b + j + 1)
                if j >= 1:
                    act.wait_ge(squares_done, NT * b + j)
                nc.scalar.activation(squares_out[:, :], fused[:, j, :], ACT.Square,
                                     accum_out=sq_sum[:, j : j + 1]).then_inc(squares_done, 1)

            def xt_hi_part(b, k, first):
                act.wait_ge(pe_xt, DT * b + k + 1)
                if k == 0 and not first:
                    act.wait_ge(pe_gx, NT * b)
                copy(xt_hi[:, k, :], x_bank(k, first)[:, :]).then_inc(xt_has_hi, 1)

            def q_hi_part(b, c):
                act.wait_ge(pe_q, CT * b + c + 1)
                copy(q_hi[:, c, :], bank[S_BANK + c][:, :]).then_inc(q_has_hi, 1)

            def u_hi_part(b, c):
                act.wait_ge(pe_u, MT * (b + 1))
                copy(u_hi[:, c, :], bank[U_BANK + c][:, :]).then_inc(u_has_hi, 1)

            def weights(g):
                act.wait_ge(pe_wt, g + 1)
                if g in WG1T:
                    dst = wg1t_hi[:, g - WG1T[0], :]
                elif g in WG2T:
                    dst = x_raw[:, g - WG2T[0], :]
                elif g in WT:
                    dst = wt_hi[:, g - WT[0], :]
                else:
                    dst = v_hi[:, g - V[0], :]
                copy(dst, weight_bank(g)[:, :]).then_inc(wt_split_hi, 1)

            def iteration(b, first, last):
                for p in range(MP):
                    for t in range(2 * p, min(2 * p + 2, MT)):
                        copy_s(b, t)
                    if p + 2 < MP:
                        mt_hi_part(b, p + 2)
                    mem_hi_part(b, p, first)
                if first:
                    for g in [*WG1T, *WG2T]:
                        weights(g)
                    copy_max(b)
                    for t in range(MT + 1):
                        softmax(b, t, first)
                        if t < 4:
                            weights(V[0] + t)
                        if not last and t - 1 in X_AT:
                            xt_hi_part(b + 1, X_AT.index(t - 1), False)
                        if not last and t == 12:
                            q_hi_part(b + 1, 0)
                            q_hi_part(b + 1, 1)
                else:
                    tanh(b - 1, 0)
                    copy_ctx(b - 1, 0)
                    copy_max(b)
                    tanh(b - 1, 1)
                    for t in range(MT + 1):
                        softmax(b, t, first)
                        if t in (0, 2, 3):
                            copy_ctx(b - 1, max(t, 1))
                        if t in (2, 3):
                            tanh(b - 1, t)
                        if t in (1, 3, 5, 7):
                            squares(b - 1, t // 2)
                        if not last and t - 1 in X_AT:
                            xt_hi_part(b + 1, X_AT.index(t - 1), False)
                        if not last and t == 13:
                            q_hi_part(b + 1, 0)
                            q_hi_part(b + 1, 1)
                if not last:
                    mt_hi_part(b + 1, 0)
                    mt_hi_part(b + 1, 1)
                for c in range(CT):
                    u_hi_part(b, c)

            act.dma_start(w_raw, w.rearrange("(k p) c -> p k c", p=P)).then_inc(in_w, 16)
            for p in range(2):
                src = mem[0, 2 * p * P : (2 * p + 2) * P, :].rearrange("(t p) c -> p t c", p=P)
                act.dma_start(mem_raw[:, 2 * p : 2 * p + 2, :], src).then_inc(in_mem[p], 16)
            xt_hi_part(0, 0, True)
            act.wait_ge(in_w, 16)
            copy(w_hi[:, :, :], w_raw).then_inc(w_split_hi, 1)
            for k in range(1, DT):
                xt_hi_part(0, k, True)
            mt_hi_part(0, 0)
            for c in range(CT):
                q_hi_part(0, c)
            mt_hi_part(0, 1)
            iteration(0, True, False)
            with act.Fori(1, B - 1) as b:
                iteration(b, False, False)
            iteration(B - 1, False, True)
            for j in range(NT):
                copy_ctx(B - 1, j)
                tanh(B - 1, j)
                if j >= 1:
                    squares(B - 1, j - 1)
            squares(B - 1, NT - 1)

        @block.vector
        def _(dve):
            def lo_part(dst, src, hi):
                return nc.vector.tensor_tensor(dst, src, hi.bitcast(F32), ALU.subtract)

            def running_max(b, t):
                dve.wait_ge(s_copied, MT * b + t + 1)
                r = rows(t)
                if t == 1:
                    a = s[0:r, 0, :]
                else:
                    a = run[0:r, :]
                    dve.wait_ge(run_done, (MT - 1) * b + t - 1)
                nc.vector.tensor_tensor(run[0:r, :], a, s[0:r, t, :], ALU.max).then_inc(run_done, 1)

            def mt_lo_part(b, p):
                dve.wait_ge(mt_has_hi, MP * b + p + 1)
                n = 2 * P if p < MP - 1 else P
                lo_part(mt_lo[:, p % 2, :, 0:n], mt_bank(p)[:, :].rearrange("p (c m) -> p c m", c=CT)[:, :, 0:n],
                        mt_hi[:, p % 2, :, 0:n]).then_inc(mt_has_lo, 1)

            def mem_lo_part(b, p):
                dve.wait_ge(mem_has_hi, MP * b + p + 1)
                ts = slice(2 * p, min(2 * p + 2, MT))
                lo_part(mem_lo[:, ts, :], mem_raw[:, ts, :], mem_hi[:, ts, :]).then_inc(mem_has_lo, 1)

            def reduce_max(b):
                dve.wait_ge(pe_max_t, b + 1)
                nc.vector.tensor_reduce(col_max[:, :], bank[S_BANK][:, :].rearrange("p (a n) -> p a n", a=NT),
                                        AX.X, ALU.max).then_inc(col_max_done, 1)
                dve.wait_ge(col_max_done, b + 1)
                nc.vector.tensor_tensor(diag[:, :, :], ident[:, :].unsqueeze(1).broadcast_to([P, NT, P]),
                                        col_max[:, :].unsqueeze(2).broadcast_to([P, NT, P]),
                                        ALU.mult).then_inc(diag_done, 1)

            def shift(b, t):
                if t == 0:
                    dve.wait_ge(max_copied, b + 1)
                r = rows(t)
                nc.vector.tensor_tensor(s[0:r, t, :], s[0:r, t, :], max_rows[0:r, :],
                                        ALU.subtract).then_inc(shifted, 1)

            def p_lo_part(b, t):
                dve.wait_ge(p_has_hi, MT * b + t + 1)
                if t >= LO_RING:
                    dve.wait_ge(pe_u, MT * b + t - LO_RING + 1)
                r = rows(t)
                lo_part(p_lo[0:r, t % LO_RING, :], p_tmp[0:r, t % TMP_RING, :], p_hi[0:r, t, :]).then_inc(p_has_lo, 1)

            def softmax(b, t):
                if t + 2 < MT:
                    shift(b, t + 2)
                p_lo_part(b, t)

            def add_bias(b, j, first):
                dve.wait_ge(pe_gx, NT * b + j + 1)
                if not first:
                    dve.wait_ge(gated, NT * (b - 1) + j + 1)
                nc.vector.tensor_tensor(gate[:, j, :], bank[S_BANK + j % 2][:, :], bias_rows[:, :],
                                        ALU.add).then_inc(gx_done, 1)

            def xt_lo_part(b, k, first=False):
                dve.wait_ge(xt_has_hi, DT * b + k + 1)
                lo_part(xt_lo[:, k, :], x_bank(k, first)[:, :], xt_hi[:, k, :]).then_inc(xt_has_lo, 1)

            def q_lo_part(b, c):
                dve.wait_ge(q_has_hi, CT * b + c + 1)
                lo_part(q_lo[:, c, :], bank[S_BANK + c][:, :], q_hi[:, c, :]).then_inc(q_has_lo, 1)

            def u_lo_part(b, c):
                dve.wait_ge(u_has_hi, CT * b + c + 1)
                lo_part(u_lo[:, c, :], bank[U_BANK + c][:, :], u_hi[:, c, :]).then_inc(u_has_lo, 1)

            def reciprocal(b):
                dve.wait_ge(pe_sum, b + 1)
                nc.vector.reciprocal(r_sum[:, :], bank[S_BANK + 1][:, 0:NT]).then_inc(r_first, 1)
                dve.wait_ge(r_first, b + 1)
                nc.vector.tensor_scalar(r_half[:, :], r_sum[:, :], 0.5, None, ALU.mult).then_inc(r_done, 1)

            def gate_input(b, j):
                dve.wait_ge(pe_g, NT * b + j + 1)
                nc.vector.scalar_tensor_tensor(gate[:, j, :], bank[G_BANK + j % 2][:, :], r_sum[:, j : j + 1],
                                               gate[:, j, :], ALU.mult, ALU.add).then_inc(z_done, 1)

            def gate_ctx(b, j):
                dve.wait_ge(tanh_done, NT * b + j + 1)
                dve.wait_ge(ctx_copied, NT * b + j + 1)
                nc.vector.scalar_tensor_tensor(fused[:, j, :], gate[:, j, :], 1.0, fused[:, j, :],
                                               ALU.add, ALU.mult).then_inc(gated, 1)

            def add_x(b, j):
                dve.wait_ge(gated, NT * b + j + 1)
                dve.wait_ge(in_x_again[j % 2], 16 * (2 * b + j // 2 + 1))
                nc.vector.tensor_tensor(fused[:, j, :], fused[:, j, :], x_again[:, j % 2, :],
                                        ALU.add).then_inc(fused_done, 1)

            def rms(b):
                count = [NEWTON_OPS * b]

                def link(instruction):
                    count[0] = count[0] + 1
                    instruction.then_inc(newton, 1)
                    dve.wait_ge(newton, count[0])

                dve.wait_ge(squares_done, NT * (b + 1))
                link(nc.vector.tensor_scalar(mean_sq[:, :], sq_sum[:, :], 1.0 / D, EPS, ALU.mult, ALU.add))
                link(nc.vector.tensor_scalar(r_rms[:, :].bitcast(I32), mean_sq[:, :].bitcast(I32), -0.5, RSQRT_MAGIC,
                                             ALU.mult, ALU.add))
                for _ in range(NEWTON_STEPS):
                    link(nc.vector.tensor_tensor(nw_a[:, :], r_rms[:, :], mean_sq[:, :], ALU.mult))
                    link(nc.vector.scalar_tensor_tensor(nw_b[:, :], nw_a[:, :], -0.5, r_rms[:, :], ALU.mult, ALU.mult))
                    link(nc.vector.scalar_tensor_tensor(r_rms[:, :], nw_b[:, :], 1.5, r_rms[:, :], ALU.add, ALU.mult))

            def output(b, j):
                nc.vector.scalar_tensor_tensor(fused[:, j, :], fused[:, j, :], r_rms[:, j : j + 1], norm_rows[:, :],
                                               ALU.mult, ALU.mult).then_inc(out_done, 1)

            def weights(g):
                dve.wait_ge(wt_split_hi, g + 1)
                if g in WG1T:
                    hi, lo = wg1t_hi[:, g - WG1T[0], :], wg1t_lo[:, g - WG1T[0], :]
                elif g in WT:
                    hi, lo = wt_hi[:, g - WT[0], :], wt_lo[:, g - WT[0], :]
                else:
                    hi, lo = v_hi[:, g - V[0], :], v_lo[:, g - V[0], :]
                lo_part(lo, weight_bank(g)[:, :], hi).then_inc(wt_split_lo, 1)

            def iteration(b, first, last):
                for p in range(MP):
                    for t in range(2 * p, min(2 * p + 2, MT)):
                        if t >= 1:
                            running_max(b, t)
                    if p + 2 < MP:
                        mt_lo_part(b, p + 2)
                    mem_lo_part(b, p)
                if first:
                    dve.wait_ge(in_rows, 32)
                    for g in WG1T:
                        weights(g)
                    reduce_max(b)
                    shift(b, 0)
                    shift(b, 1)
                    for t in range(MT):
                        softmax(b, t)
                        if t < 4:
                            weights(V[0] + t)
                        if 2 <= t < 2 + NT:
                            add_bias(b, t - 2, first)
                        if t in X_AT:
                            xt_lo_part(b + 1, X_AT.index(t))
                else:
                    reciprocal(b - 1)
                    gate_input(b - 1, 0)
                    reduce_max(b)
                    gate_ctx(b - 1, 0)
                    gate_input(b - 1, 1)
                    add_x(b - 1, 0)
                    shift(b, 0)
                    shift(b, 1)
                    for t in range(MT):
                        if t in (1, 2):
                            gate_input(b - 1, t + 1)
                        if 3 <= t < 3 + NT:
                            add_bias(b, t - 3, first)
                        if t in (0, 2, 4):
                            gate_ctx(b - 1, 1 + t // 2)
                        if t in (1, 3, 5):
                            add_x(b - 1, (t + 1) // 2)
                        softmax(b, t)
                        if not last and t in X_AT:
                            xt_lo_part(b + 1, X_AT.index(t))
                    rms(b - 1)
                    for j in range(NT):
                        output(b - 1, j)
                if not last:
                    q_lo_part(b + 1, 0)
                    q_lo_part(b + 1, 1)
                    mt_lo_part(b + 1, 0)
                    mt_lo_part(b + 1, 1)
                for c in range(CT):
                    u_lo_part(b, c)

            nc.vector.memset(ones[:, :], 1.0).then_inc(ready_ones, 1)
            nc.vector.memset(mem_raw[:, MT - 1, :], 0.0).then_inc(ready_pad, 1)
            xt_lo_part(0, 0, True)
            dve.wait_ge(w_split_hi, 1)
            lo_part(w_lo[:, :, :], w_raw, w_hi[:, :, :]).then_inc(w_split_lo, 1)
            for k in range(1, DT):
                xt_lo_part(0, k, True)
            mt_lo_part(0, 0)
            for c in range(CT):
                q_lo_part(0, c)
            mt_lo_part(0, 1)
            iteration(0, True, False)
            with dve.Fori(1, B - 1) as b:
                iteration(b, False, False)
            iteration(B - 1, False, True)
            reciprocal(B - 1)
            for j in range(NT):
                gate_input(B - 1, j)
                if j >= 1:
                    gate_ctx(B - 1, j - 1)
                    add_x(B - 1, j - 1)
            gate_ctx(B - 1, NT - 1)
            add_x(B - 1, NT - 1)
            rms(B - 1)
            for j in range(NT):
                output(B - 1, j)

        @block.gpsimd
        def _(pool):
            def add_p(b, t, first):
                pool.wait_ge(exp_done, MT * b + t + 1)
                r = rows(t)
                if t == 1:
                    if not first:
                        pool.wait_ge(pe_sum, b)
                    a = p_tmp[0:r, 0, :]
                else:
                    pool.wait_ge(p_added, (MT - 1) * b + t - 1)
                    a = psum_rows[0:r, :]
                nc.gpsimd.tensor_tensor(psum_rows[0:r, :], a, p_tmp[0:r, t % TMP_RING, :], ALU.add).then_inc(p_added, 1)

            nc.gpsimd.memset(ident[:, :], 0.0).then_inc(cleared, 1)
            pool.wait_ge(cleared, 1)
            nc.gpsimd.affine_select(out=ident[:, :], in_=ident[:, :], compare_op=ALU.not_equal, fill=1.0, base=0,
                                    pattern=[[-1, P]], channel_multiplier=1).then_inc(ready_ident, 1)
            for t in range(1, MT):
                add_p(0, t, True)
            with pool.Fori(1, B) as b:
                for t in range(1, MT):
                    add_p(b, t, False)


_INS = ["x", "ctx_1024", "L0_xattn_W_mem", "L0_xattn_W_gate", "L0_xattn_b_gate", "L0_xattn_norm_w"]
_OUTS = [((8, 512, 512), "float32")]


def kernel(**inputs):
    import numpy as _np
    import concourse.bacc as _bacc
    from concourse import mybir as _mybir
    from concourse.bass_utils import run_bass_kernel_spmd as _run

    nc = _bacc.Bacc("TRN2", target_bir_lowering=False, num_devices=1, dynamic_dma_scratch_size=1024)
    arrays, args = {}, []
    for name in _INS:
        a = _np.ascontiguousarray(inputs[name])
        arrays[f"in_{name}_dram"] = a
        args.append(nc.dram_tensor(f"in_{name}_dram", a.shape, _mybir.dt.from_np(a.dtype), kind="ExternalInput").ap())
    for i, (shape, dtype) in enumerate(_OUTS):
        dt = _mybir.dt.from_np(_np.dtype(dtype))
        args.append(nc.dram_tensor(f"out_{i}_dram", shape, dt, kind="ExternalOutput").ap())
    xattn_kernel(nc, *args)
    r = _run(nc, [arrays], core_ids=[0])
    return r.results[0]["out_0_dram"]
```

```python
from contextlib import ExitStack

import concourse.bass as bass
from concourse import mybir

ALU = mybir.AluOpType
ACT = mybir.ActivationFunctionType
AX = mybir.AxisListType
F32 = mybir.dt.float32
F32R = mybir.dt.float32r
I32 = mybir.dt.int32

P = 128
BLOCK = 32
BLOCKS = P // BLOCK
EPS = 1e-6
RSQRT_MAGIC = float(0x5F3759DF)
NEWTON_STEPS = 3


def xattn_kernel(nc: bass.Bass, x, mem, w, wg, b_gate, norm_w, out):
    B, N, D = x.shape
    _, M, C = mem.shape
    NT = N // P
    DT = D // P
    CT = C // P
    MT = -(-M // P)
    LAST = M - (MT - 1) * P
    MP = -(-MT // 2)
    TMP_RING = 4
    LO_RING = 10
    RAW_PAIRS = 4
    ROW_BLOCKS = -(-M // BLOCK)
    DA = D // BLOCKS
    CA = C // BLOCKS
    assert N == 512 and D == 512 and C == 256 and MT % 2 == 1 and M % BLOCK == 1

    def rows(t):
        return P if t < MT - 1 else LAST

    with ExitStack() as ctx:

        def sb(name, shape, dt=F32):
            return ctx.enter_context(nc.sbuf_tensor(name, shape, dt))

        def sem(name):
            return ctx.enter_context(nc.semaphore(name))

        s_offset = -(-nc.sbuf_base // 32) * 32
        s = sb("s", [P, MT, N])
        p_hi = nc.alloc_sbuf_tensor_at("p_hi", [P, MT, N], F32R, offset=s_offset)
        p_tmp = sb("p_tmp", [P, TMP_RING, N])
        p_lo = sb("p_lo", [P, LO_RING, N], F32R)
        mem_raw = sb("mem_raw", [P, 2 * RAW_PAIRS, C])
        mem_blocks = sb("mem_blocks", [P, ROW_BLOCKS, CA])
        mem_hi = sb("mem_hi", [P, MT, C], F32R)
        mem_lo = sb("mem_lo", [P, MT, C], F32R)
        mt_hi = sb("mt_hi", [P, 2, CT, 2 * P], F32R)
        mt_lo = sb("mt_lo", [P, 2, CT, 2 * P], F32R)
        x_raw = sb("x_raw", [P, NT, D])
        x_blocks = x_raw[:, :, :].rearrange("p t d -> p (t d)").rearrange("p (r f) -> p r f", f=DA)
        xt_hi = sb("xt_hi", [P, DT, N], F32R)
        xt_lo = sb("xt_lo", [P, DT, N], F32R)
        q_hi = sb("q_hi", [P, CT, N], F32R)
        q_lo = sb("q_lo", [P, CT, N], F32R)
        u_hi = sb("u_hi", [P, CT, N], F32R)
        u_lo = sb("u_lo", [P, CT, N], F32R)
        gate = sb("gate", [P, NT, D])
        fused = sb("fused", [P, NT, D])
        squares_out = sb("squares_out", [P, D])
        x_again = sb("x_again", [P, 2, D])
        w_hi = sb("w_hi", [P, DT, C], F32R)
        w_lo = sb("w_lo", [P, DT, C], F32R)
        wt_hi = sb("wt_hi", [P, CT, D], F32R)
        wt_lo = sb("wt_lo", [P, CT, D], F32R)
        wg1t_hi = sb("wg1t_hi", [P, DT, D], F32R)
        wg1t_lo = sb("wg1t_lo", [P, DT, D], F32R)
        v_hi = sb("v_hi", [P, CT, D], F32R)
        v_lo = sb("v_lo", [P, CT, D], F32R)
        bias_rows = sb("bias_rows", [P, D])
        norm_rows = sb("norm_rows", [P, D])
        run = sb("run", [P, N])
        psum_rows = sb("psum_rows", [P, N])
        ident = sb("ident", [P, P])
        ones = sb("ones", [P, 1])
        col_max = sb("col_max", [P, NT])
        r_sum = sb("r_sum", [P, NT])
        r_half = sb("r_half", [P, NT])
        sq_sum = sb("sq_sum", [P, NT])
        mean_sq = sb("mean_sq", [P, NT])
        r_rms = sb("r_rms", [P, NT])
        nw_a = sb("nw_a", [P, NT])
        nw_b = sb("nw_b", [P, NT])
        w_raw = x_again[:, :, :].rearrange("p a (k c) -> p (a k) c", c=C)
        wg_raw = [
            (gate, fused)[i // 2][:, 2 * (i % 2) : 2 * (i % 2) + 2, :].rearrange("p a f -> p (a f)")
            for i in range(DT)
        ]

        bank = [ctx.enter_context(nc.psum_tensor(f"bank{i}", [P, 512], F32)) for i in range(8)]
        U_BANK, S_BANK, MAX_BANK, G_BANK, CTX_BANK = 0, 2, 3, 4, 6
        QX_BANKS = (2, 4)

        def x_bank(k, first):
            return bank[(6, 7, 3, 0)[k] if first else CTX_BANK + k % 2]

        def tile_columns(ap, k, tiles):
            if len(ap.shape) == 2:
                return ap.rearrange("p (f t) -> p t f", t=tiles)[:, k, :]
            return ap.rearrange("p a (f t) -> p a t f", t=tiles)[:, :, k, :]

        def s_bank(t):
            return bank[S_BANK + t % 3]

        def mt_bank(p):
            return bank[5 + p % 2]

        in_x, in_w, in_wg, in_rows = sem("in_x"), sem("in_w"), sem("in_wg"), sem("in_rows")
        in_x_first = [sem(f"in_x_first{k}") for k in range(NT)]
        in_mem = [sem(f"in_mem{p}") for p in range(MP)]
        in_blocks = [sem(f"in_blocks{g}") for g in range(2)]
        in_x_again = [sem(f"in_x_again{i}") for i in range(2)]
        fused_free = [sem(f"fused_free{j}") for j in range(NT)]
        cleared, ready_ident, ready_ones, ready_pad = (
            sem("cleared"), sem("ready_ident"), sem("ready_ones"), sem("ready_pad"))
        w_split_hi, w_split_lo = sem("w_split_hi"), sem("w_split_lo")
        pe_wt, wt_split_hi, wt_split_lo = sem("pe_wt"), sem("wt_split_hi"), sem("wt_split_lo")
        pe_mt, pe_s, pe_max_t, pe_max_rows = sem("pe_mt"), sem("pe_s"), sem("pe_max_t"), sem("pe_max_rows")
        pe_sum, pe_ctx, pe_g, pe_gx = sem("pe_sum"), sem("pe_ctx"), sem("pe_g"), sem("pe_gx")
        pe_xt, pe_q, pe_u = sem("pe_xt"), sem("pe_q"), sem("pe_u")
        pe_u_first = sem("pe_u_first")
        s_copied, mt_has_hi, mem_has_hi = sem("s_copied"), sem("mt_has_hi"), sem("mem_has_hi")
        exp_done, p_has_hi, xt_has_hi = sem("exp_done"), sem("p_has_hi"), sem("xt_has_hi")
        q_has_hi, u_has_hi = sem("q_has_hi"), sem("u_has_hi")
        ctx_copied, tanh_done, squares_done = sem("ctx_copied"), sem("tanh_done"), sem("squares_done")
        xt_done, mt_done = sem("xt_done"), sem("mt_done")
        run_done, mt_has_lo, mem_has_lo = sem("run_done"), sem("mt_has_lo"), sem("mem_has_lo")
        col_max_done, shifted = sem("col_max_done"), sem("shifted")
        p_has_lo, xt_has_lo, q_has_lo = sem("p_has_lo"), sem("xt_has_lo"), sem("q_has_lo")
        u_has_lo, gx_done, r_first, r_done = sem("u_has_lo"), sem("gx_done"), sem("r_first"), sem("r_done")
        z_done, gated, fused_done = sem("z_done"), sem("gated"), sem("fused_done")
        newton, out_done = sem("newton"), sem("out_done")
        normed, tail_done = sem("normed"), sem("tail_done")
        p_added = sem("p_added")

        NEWTON_OPS = 2 + 3 * NEWTON_STEPS
        WT, WG2T, WG1T, V = range(0, 2), range(2, 6), range(6, 10), range(10, 12)
        FUSED_FREED_AT = [(V[0], 0), (V[0], 1), (V[0], 2), (V[1], 0)]
        WG2T_AT = [5, 7, 9, 11]

        X_AT = [6, 7, 9, 10]
        X_BLOCKS_AT = [4, 5, 7, 8]
        MEM_BLOCKS_AT = [10, 11]
        QUERY_AT = 9
        ADD_AT = [1, 3, 11]
        SPLIT_BY_SCORES = {0: [0], 2: [1], 4: [2], 5: [3], 6: [4, 5]}
        SPLIT_BY_SOFTMAX = {5: [6]}

        def mem_in_bank(engine, b, p):
            if isinstance(b, int) and b == 0 and p < 2:
                engine.wait_ge(pe_mt, p + 1)
            else:
                engine.wait_ge(mt_done, MP * b + p - 1)

        def mem_pair(p):
            n, slot = min(2, MT - 2 * p), 2 * (p % RAW_PAIRS)
            return slice(2 * p, 2 * p + n), slice(slot, slot + n), (P if n == 2 else LAST)

        def weight_bank(g):
            return bank[(1, 7, 0, 1, 7, 0, 4, 5, 6, 7, 0, 1)[g]]

        block = ctx.enter_context(nc.Block())

        @block.sync
        def _(sp):
            def load_x(b):
                for a in range(BLOCKS):
                    src = x[b, :, a * DA : (a + 1) * DA].rearrange("(r j) f -> j r f", j=BLOCK)
                    sp.dma_start(x_blocks[a * BLOCK : (a + 1) * BLOCK, :, :], src).then_inc(in_x, 16)

            def load_mem_blocks(b, g):
                r0, r1 = ((0, 4 * P // BLOCK), (4 * P // BLOCK, ROW_BLOCKS - 1))[g]
                for a in range(BLOCKS):
                    src = mem[b, r0 * BLOCK : r1 * BLOCK, a * CA : (a + 1) * CA].rearrange("(r j) f -> j r f", j=BLOCK)
                    sp.dma_start(mem_blocks[a * BLOCK : (a + 1) * BLOCK, r0:r1, :], src).then_inc(in_blocks[g], 16)
                if g == 1:
                    sp.dma_start(mem_blocks[0:P:BLOCK, r1, :], mem[b, M - 1, :].rearrange("(a f) -> a f", f=CA)
                                 ).then_inc(in_blocks[g], 16)

            def load_mem(b, p):
                slot = 2 * (p % RAW_PAIRS)
                if p < MP - 1:
                    src = mem[b, 2 * p * P : (2 * p + 2) * P, :].rearrange("(t p) c -> p t c", p=P)
                    sp.dma_start(mem_raw[:, slot : slot + 2, :], src).then_inc(in_mem[p], 16)
                else:
                    sp.dma_start(mem_raw[0:LAST, slot, :], mem[b, (MT - 1) * P : M, :]).then_inc(in_mem[p], 16)

            def load_mem_again(b, p):
                behind = p - RAW_PAIRS if p >= RAW_PAIRS else min(p + RAW_PAIRS, MP - 1) - MP
                sp.wait_ge(mem_has_lo, MP * b + behind + 1)
                load_mem(b, p)

            def load_x_again(b, j):
                sp.dma_start(x_again[:, j % 2, :], x[b, j * P : (j + 1) * P, :]).then_inc(in_x_again[j % 2], 16)

            def store(b, j):
                sp.wait_ge(out_done, NT * b + j + 1)
                sp.dma_start(out[b, j * P : (j + 1) * P, :], fused[:, j, :]).then_inc(fused_free[j], 16)

            def iteration(b, last):
                if not last:
                    sp.wait_ge(xt_done, DT * b)
                    load_x(b + 1)
                    sp.wait_ge(mt_done, MP * b)
                    load_mem_blocks(b + 1, 0)
                load_x_again(b - 1, 0)
                load_x_again(b - 1, 1)
                for p in range(RAW_PAIRS, MP):
                    load_mem_again(b, p)
                if not last:
                    sp.wait_ge(mt_done, MP * b + MP - 2)
                    load_mem_blocks(b + 1, 1)
                for j in range(2, NT):
                    sp.wait_ge(fused_done, NT * (b - 1) + j - 1)
                    load_x_again(b - 1, j)
                if not last:
                    for p in range(RAW_PAIRS):
                        load_mem_again(b + 1, p)
                for j in range(NT):
                    store(b - 1, j)

            for j in range(NT):
                sp.dma_start(x_raw[:, j, :], x[0, j * P : (j + 1) * P, :]).then_inc(in_x_first[j], 16)
            for p in range(2):
                load_mem(0, p)
            sp.wait_ge(ready_pad, 1)
            load_mem_blocks(0, 1)
            for p in range(2, RAW_PAIRS):
                load_mem(0, p)
            for i in range(DT):
                sp.dma_start(wg_raw[i], wg[i * P : (i + 1) * P, :]).then_inc(in_wg, 16)
            sp.dma_start(bias_rows[:, :], b_gate.partition_broadcast(P)).then_inc(in_rows, 16)
            sp.dma_start(norm_rows[:, :], norm_w.partition_broadcast(P)).then_inc(in_rows, 16)

            load_mem_blocks(1, 0)
            for p in range(RAW_PAIRS, MP):
                load_mem_again(0, p)
            sp.wait_ge(mt_done, MP - 2)
            load_mem_blocks(1, 1)
            sp.wait_ge(pe_wt, V[-1] + 1)
            load_x(1)
            for p in range(RAW_PAIRS):
                load_mem_again(1, p)
            with sp.Fori(1, B - 1) as b:
                iteration(b, False)
            iteration(B - 1, True)
            load_x_again(B - 1, 0)
            load_x_again(B - 1, 1)
            for j in range(2, NT):
                sp.wait_ge(fused_done, NT * (B - 1) + j - 1)
                load_x_again(B - 1, j)
            for j in range(NT):
                if 0 < j < NT - 1:
                    sp.wait_ge(tail_done, j)
                else:
                    sp.wait_ge(out_done, NT * (B - 1) + (1 if j == 0 else 2))
                sp.dma_start(out[B - 1, j * P : (j + 1) * P, :], fused[:, j, :]).then_inc(fused_free[j], 16)
            for j in range(NT):
                sp.wait_ge(fused_free[j], 16 * (B + 1))

        @block.tensor
        def _(pe):
            def product(dst, terms, start=True, stop=True):
                n = len(terms)
                for i, (a_hi, a_lo, b_hi, b_lo) in enumerate(terms):
                    nc.tensor.matmul(dst, a_hi, b_hi, start=(start and i == 0), stop=False)
                    nc.tensor.matmul(dst, a_hi, b_lo, start=False, stop=False)
                    last = nc.tensor.matmul(dst, a_lo, b_hi, start=False, stop=(stop and i == n - 1))
                return last

            def transpose_first_x():
                for j in range(NT):
                    pe.wait_ge(in_x_first[j], 16)
                    for k in range(DT):
                        last = nc.tensor.transpose(x_bank(k, True)[:, j * P : (j + 1) * P],
                                                   tile_columns(x_raw[:, j, :], k, DT), ident[:, :])
                        if j == NT - 1:
                            last.then_inc(pe_xt, 1)

            def query(c, ks):
                last = product(bank[QX_BANKS[c]][:, :], [
                    (w_hi[:, k, c * P : (c + 1) * P], w_lo[:, k, c * P : (c + 1) * P], xt_hi[:, k, :], xt_lo[:, k, :])
                    for k in ks], start=(ks[0] == 0), stop=(ks[-1] == DT - 1))
                if ks[-1] == DT - 1:
                    last.then_inc(pe_q, 1)

            def transpose_first_mem(p):
                pe.wait_ge(in_mem[p], 16)
                for c in range(CT):
                    for t in range(2 * p, 2 * p + 2):
                        at = c * 2 * P + (t % 2) * P
                        last = nc.tensor.transpose(mt_bank(p)[:, at : at + P], tile_columns(mem_raw[:, t, :], c, CT),
                                                   ident[:, :])
                last.then_inc(pe_mt, 1)

            def score(b, t):
                p, m = t // 2, (t % 2) * P
                pe.wait_ge(mt_has_lo, MP * b + p + 1)
                if t >= 3:
                    pe.wait_ge(s_copied, MT * b + t - 2)
                r = rows(t)
                for c in range(CT):
                    if t == 0:
                        pe.wait_ge(q_has_lo, CT * b + c + 1)
                    last = product(s_bank(t)[0:r, :], [
                        (mt_hi[:, p % 2, c, m : m + r], mt_lo[:, p % 2, c, m : m + r], q_hi[:, c, :], q_lo[:, c, :])
                    ], start=(c == 0), stop=(c == CT - 1))
                last.then_inc(pe_s, 1)

            def scores(b, first):
                for t in range(MT):
                    score(b, t)
                    if first and t in WG2T_AT:
                        if t == WG2T_AT[0]:
                            pe.wait_ge(in_wg, 16 * DT)
                        weights(WG2T[WG2T_AT.index(t)])

            def transpose_max(b):
                pe.wait_ge(run_done, (MT - 1) * (b + 1))
                pe.wait_ge(s_copied, MT * (b + 1))
                for j in range(NT):
                    last = nc.tensor.transpose(
                        bank[S_BANK][:, j * P : (j + 1) * P], run[:, j * P : (j + 1) * P], ident[:, :])
                last.then_inc(pe_max_t, 1)

            def spread_max(b, first):
                pe.wait_ge(col_max_done, b + 1)
                if not first:
                    pe.wait_ge(r_done, b)
                for j in range(NT):
                    last = nc.tensor.transpose(bank[MAX_BANK][:, j * P : (j + 1) * P],
                                               col_max[:, j : j + 1].broadcast_to([P, P]), ident[:, :])
                last.then_inc(pe_max_rows, 1)

            def row_sums(b, behind_scores):
                pe.wait_ge(p_added, (MT - 1) * (b + 1))
                if behind_scores:
                    pe.wait_ge(s_copied, MT * (b + 1) + MT - 2)
                else:
                    pe.wait_ge(shifted, MT * (b + 1))
                for j in range(NT):
                    last = nc.tensor.matmul(bank[MAX_BANK][:, j : j + 1], psum_rows[:, j * P : (j + 1) * P],
                                            ones[:, :], start=True, stop=True)
                last.then_inc(pe_sum, 1)

            def gate_context(b, j, behind_scores):
                if j == 0:
                    if behind_scores:
                        pe.wait_ge(u_has_lo, CT * (b + 1))
                        pe.wait_ge(mt_has_lo, MP * (b + 2))
                        pe.wait_ge(s_copied, MT * (b + 1) + MT - 1)
                if j >= 2:
                    pe.wait_ge(z_done, NT * b + j - 1)
                n = slice(j * P, (j + 1) * P)
                for c in range(CT):
                    if j == 0 and not behind_scores:
                        pe.wait_ge(u_has_lo, CT * b + c + 1)
                    last = product(bank[G_BANK + j % 2][:, :], [
                        (u_hi[:, c, n], u_lo[:, c, n], v_hi[:, c, :], v_lo[:, c, :])
                    ], start=(c == 0), stop=(c == CT - 1))
                last.then_inc(pe_g, 1)

            def context(b, j):
                if j >= 2:
                    pe.wait_ge(ctx_copied, NT * b + j - 1)
                n = slice(j * P, (j + 1) * P)
                product(bank[CTX_BANK + j % 2][:, :], [
                    (u_hi[:, c, n], u_lo[:, c, n], wt_hi[:, c, :], wt_lo[:, c, :]) for c in range(CT)
                ]).then_inc(pe_ctx, 1)

            def gate_x(b, j, first):
                if j == 0:
                    pe.wait_ge(col_max_done, b + 1)
                elif j == 1:
                    if not first:
                        pe.wait_ge(z_done, NT * b - 1)
                else:
                    pe.wait_ge(gx_done, NT * b + j - 1)
                n = slice(j * P, (j + 1) * P)
                product(bank[QX_BANKS[j % 2]][:, :], [
                    (xt_hi[:, k, n], xt_lo[:, k, n], wg1t_hi[:, k, :], wg1t_lo[:, k, :]) for k in range(DT)
                ]).then_inc(pe_gx, 1)

            def weighted(b, t):
                if t % 2 == 0:
                    pe.wait_ge(mem_has_lo, MP * b + t // 2 + 1)
                pe.wait_ge(p_has_lo, MT * b + t + 1)
                r = rows(t)
                for c in range(CT):
                    cs = slice(c * P, (c + 1) * P)
                    dst = bank[U_BANK + c][:, :]
                    nc.tensor.matmul(dst, mem_hi[0:r, t, cs], p_hi[0:r, t, :], start=(t == 0), stop=False)
                    nc.tensor.matmul(dst, mem_hi[0:r, t, cs], p_lo[0:r, t % LO_RING, :], start=False, stop=False)
                    last = nc.tensor.matmul(dst, mem_lo[0:r, t, cs], p_hi[0:r, t, :], start=False, stop=(t == MT - 1))
                    if c == 0 and t == MT - 1:
                        last.then_inc(pe_u_first, 1)
                last.then_inc(pe_u, 1)

            def weights(g):
                if g in WG2T and g > WG2T[0]:
                    if g < WG2T[-1]:
                        pe.wait_ge(wt_split_lo, g - WG2T[0])
                    else:
                        pe.wait_ge(wt_split_hi, WG2T[0] + 1)
                dst = weight_bank(g)
                if g in V:
                    c = g - V[0]
                    for k in range(DT):
                        last = nc.tensor.matmul(dst[:, :], w_raw[:, k, c * P : (c + 1) * P], x_raw[:, k, :],
                                                start=(k == 0), stop=(k == DT - 1))
                        if (g, k) in FUSED_FREED_AT:
                            last.then_inc(fused_free[FUSED_FREED_AT.index((g, k))], 16)
                else:
                    for i in range(DT):
                        if g in WT:
                            to = tile_columns(dst[:, :], i, DT)
                            src = w_raw[:, i, (g - WT[0]) * P : (g - WT[0] + 1) * P]
                        else:
                            to = dst[:, i * P : (i + 1) * P]
                            half, k = (0, g - WG1T[0]) if g in WG1T else (1, g - WG2T[0])
                            src = tile_columns(wg_raw[i][:, half * D : (half + 1) * D], k, DT)
                        last = nc.tensor.transpose(to, src, ident[:, :])
                last.then_inc(pe_wt, 1)

            def iteration(b, first, last):
                scores(b, first)
                if first:
                    pe.wait_ge(mt_has_lo, MP)
                    pe.wait_ge(s_copied, MT - 1)
                    pe.wait_ge(wt_split_hi, WG2T[-1] + 1)
                    for g in WG1T:
                        weights(g)
                    transpose_max(b)
                    weights(V[0])
                    spread_max(b, first)
                    weights(V[1])
                    pe.wait_ge(wt_split_lo, len(WT) + len(WG1T))
                else:
                    row_sums(b - 1, True)
                    gate_context(b - 1, 0, True)
                    transpose_max(b)
                    context(b - 1, 0)
                    gate_context(b - 1, 1, True)
                    spread_max(b, first)
                    context(b - 1, 1)
                    for j in (2, 3):
                        gate_context(b - 1, j, True)
                        context(b - 1, j)
                for j in range(NT):
                    gate_x(b, j, first)
                if first:
                    pe.wait_ge(wt_split_lo, len(WT) + len(WG1T) + len(V))
                else:
                    pe.wait_ge(u_has_lo, CT * b)
                for t in range(MT):
                    weighted(b, t)
                    if t == QUERY_AT and not last:
                        pe.wait_ge(xt_has_lo, DT * (b + 2))
                        pe.wait_ge(gx_done, NT * (b + 1))
                        for c in range(CT):
                            query(c, range(DT))

            pe.wait_ge(ready_ident, 1)
            pe.wait_ge(ready_ones, 1)
            transpose_first_x()
            transpose_first_mem(0)
            pe.wait_ge(in_w, 16)
            weights(WT[0])
            pe.wait_ge(w_split_lo, CT)
            for k in range(DT):
                pe.wait_ge(xt_has_lo, k + 1)
                query(0, [k])
                if k == 0:
                    query(1, [k])
            query(1, range(1, DT))
            transpose_first_mem(1)
            weights(WT[1])
            iteration(0, True, False)
            with pe.Fori(1, B - 1) as b:
                iteration(b, False, False)
            iteration(B - 1, False, True)
            row_sums(B - 1, False)
            for j in range(NT):
                gate_context(B - 1, j, False)
                context(B - 1, j)

        @block.scalar
        def _(act):
            def copy(dst, src):
                return nc.scalar.activation(dst, src, ACT.Copy)

            def mt_hi_part(b, p):
                mem_in_bank(act, b, p)
                if p >= 2:
                    act.wait_ge(pe_s, MT * b + 2 * p - 2)
                elif not (isinstance(b, int) and b == 0):
                    act.wait_ge(pe_s, MT * b)
                n = 2 * P if p < MP - 1 else LAST
                copy(mt_hi[:, p % 2, :, 0:n], mt_bank(p)[:, :].rearrange("p (c m) -> p c m", c=CT)[:, :, 0:n]
                     ).then_inc(mt_has_hi, 1)

            def mem_hi_part(b, p, first):
                if p == 0 and not first:
                    act.wait_ge(pe_u, MT * b)
                act.wait_ge(in_mem[p], 16 * (b + 1))
                ts, raw, r = mem_pair(p)
                copy(mem_hi[0:r, ts, :], mem_raw[0:r, raw, :]).then_inc(mem_has_hi, 1)

            def copy_s(b, t):
                act.wait_ge(pe_s, MT * b + t + 1)
                copy(s[0 : rows(t), t, :], s_bank(t)[0 : rows(t), :]).then_inc(s_copied, 1)

            def exp(b, t, first):
                act.wait_ge(shifted, MT * b + t + 1)
                if t >= TMP_RING:
                    act.wait_ge(p_has_lo, MT * b + t - TMP_RING + 1)
                    act.wait_ge(p_added, (MT - 1) * b + max(t - TMP_RING, 1))
                elif not first:
                    act.wait_ge(p_has_lo, MT * b)
                    act.wait_ge(p_added, (MT - 1) * b)
                r = rows(t)
                nc.scalar.activation(p_tmp[0:r, t % TMP_RING, :], s[0:r, t, :], ACT.Exp,
                                     scale=float(D) ** -0.5).then_inc(exp_done, 1)

            def p_hi_part(b, t):
                act.wait_ge(exp_done, MT * b + t + 1)
                r = rows(t)
                copy(p_hi[0:r, t, :], p_tmp[0:r, t % TMP_RING, :]).then_inc(p_has_hi, 1)

            def softmax(b, t, first):
                if t < MT:
                    exp(b, t, first)
                if t >= 1:
                    p_hi_part(b, t - 1)

            def copy_ctx(b, j):
                act.wait_ge(pe_ctx, NT * b + j + 1)
                if j == 0:
                    act.wait_ge(r_done, b + 1)
                act.wait_ge(fused_free[j], 16 * (b + 1))
                nc.scalar.activation(fused[:, j, :], bank[CTX_BANK + j % 2][:, :], ACT.Copy,
                                     scale=r_half[:, j : j + 1]).then_inc(ctx_copied, 1)

            def tanh(b, j):
                act.wait_ge(z_done, NT * b + j + 1)
                nc.scalar.activation(gate[:, j, :], gate[:, j, :], ACT.Tanh, scale=0.5).then_inc(tanh_done, 1)

            def squares(b, j):
                act.wait_ge(fused_done, NT * b + j + 1)
                if j >= 1:
                    act.wait_ge(squares_done, NT * b + j)
                nc.scalar.activation(squares_out[:, :], fused[:, j, :], ACT.Square,
                                     accum_out=sq_sum[:, j : j + 1]).then_inc(squares_done, 1)

            def xt_hi_part(b, k, first):
                if first:
                    act.wait_ge(pe_xt, k + 1)
                else:
                    act.wait_ge(xt_done, DT * (b - 1) + k + 1)
                if k == 0 and not first:
                    act.wait_ge(pe_gx, NT * b)
                copy(xt_hi[:, k, :], x_bank(k, first)[:, :]).then_inc(xt_has_hi, 1)

            def q_hi_part(b, c):
                act.wait_ge(pe_q, CT * b + c + 1)
                copy(q_hi[:, c, :], bank[QX_BANKS[c]][:, :]).then_inc(q_has_hi, 1)

            def u_hi_part(b, c):
                if c == 0:
                    act.wait_ge(pe_u_first, b + 1)
                else:
                    act.wait_ge(pe_u, MT * (b + 1))
                copy(u_hi[:, c, :], bank[U_BANK + c][:, :]).then_inc(u_has_hi, 1)

            def weights(g):
                act.wait_ge(pe_wt, g + 1)
                if g in WG1T:
                    dst = wg1t_hi[:, g - WG1T[0], :]
                elif g in WG2T:
                    dst = x_raw[:, g - WG2T[0], :]
                elif g in WT:
                    dst = wt_hi[:, g - WT[0], :]
                else:
                    dst = v_hi[:, g - V[0], :]
                copy(dst, weight_bank(g)[:, :]).then_inc(wt_split_hi, 1)

            def iteration(b, first, last):
                for p in range(MP):
                    copy_s(b, 2 * p)
                    if p + 2 < MP:
                        mt_hi_part(b, p + 2)
                    if 2 * p + 1 < MT:
                        copy_s(b, 2 * p + 1)
                    for t in (2 * p, 2 * p + 1):
                        if first and t in WG2T_AT:
                            weights(WG2T[WG2T_AT.index(t)])
                    for q in SPLIT_BY_SCORES.get(p, []):
                        mem_hi_part(b, q, first)
                if first:
                    for g in [*WG1T, V[0]]:
                        weights(g)
                    for t in range(MT + 1):
                        for q in SPLIT_BY_SOFTMAX.get(t, []):
                            mem_hi_part(b, q, first)
                        softmax(b, t, first)
                        if t == 1:
                            weights(V[1])
                        if not last and t - 1 in X_AT:
                            xt_hi_part(b + 1, X_AT.index(t - 1), False)
                        if not last and t == 12:
                            q_hi_part(b + 1, 0)
                            q_hi_part(b + 1, 1)
                else:
                    tanh(b - 1, 0)
                    copy_ctx(b - 1, 0)
                    tanh(b - 1, 1)
                    for t in range(MT + 1):
                        for q in SPLIT_BY_SOFTMAX.get(t, []):
                            mem_hi_part(b, q, first)
                        softmax(b, t, first)
                        if t in (0, 2, 3):
                            copy_ctx(b - 1, max(t, 1))
                        if t in (2, 3):
                            tanh(b - 1, t)
                        if t == 1:
                            squares(b - 1, 0)
                        if t - 2 in ADD_AT:
                            squares(b - 1, ADD_AT.index(t - 2) + 1)
                        if not last and t - 1 in X_AT:
                            xt_hi_part(b + 1, X_AT.index(t - 1), False)
                        if not last and t == 13:
                            q_hi_part(b + 1, 0)
                            q_hi_part(b + 1, 1)
                if not last:
                    mt_hi_part(b + 1, 0)
                    mt_hi_part(b + 1, 1)
                for c in range(CT):
                    u_hi_part(b, c)

            act.dma_start(w_raw, w.rearrange("(p k) c -> p k c", k=DT)).then_inc(in_w, 16)
            act.wait_ge(in_w, 16)
            for c in range(CT):
                copy(w_hi[:, :, c * P : (c + 1) * P], tile_columns(w_raw, c, CT)).then_inc(w_split_hi, 1)
            for k in range(DT):
                xt_hi_part(0, k, True)
            mt_hi_part(0, 0)
            weights(WT[0])
            for c in range(CT):
                q_hi_part(0, c)
            mt_hi_part(0, 1)
            weights(WT[1])
            iteration(0, True, False)
            with act.Fori(1, B - 1) as b:
                iteration(b, False, False)
            iteration(B - 1, False, True)
            for j in range(NT):
                tanh(B - 1, j)
                copy_ctx(B - 1, j)
                if j >= 1:
                    squares(B - 1, j - 1)
            squares(B - 1, NT - 1)
            act.wait_ge(normed, NT - 1)
            act.wait_ge(newton, NEWTON_OPS * B)
            for j in range(1, NT - 1):
                nc.scalar.activation(fused[:, j, :], gate[:, j, :], ACT.Copy,
                                     scale=r_rms[:, j : j + 1]).then_inc(tail_done, 1)

        @block.vector
        def _(dve):
            def lo_part(dst, src, hi):
                return nc.vector.tensor_tensor(dst, src, hi.bitcast(F32), ALU.subtract)

            def running_max(b, t):
                dve.wait_ge(s_copied, MT * b + t + 1)
                r = rows(t)
                if t == 1:
                    a = s[0:r, 0, :]
                else:
                    a = run[0:r, :]
                    dve.wait_ge(run_done, (MT - 1) * b + t - 1)
                nc.vector.tensor_tensor(run[0:r, :], a, s[0:r, t, :], ALU.max).then_inc(run_done, 1)

            def mt_lo_part(b, p):
                dve.wait_ge(mt_has_hi, MP * b + p + 1)
                n = 2 * P if p < MP - 1 else LAST
                lo_part(mt_lo[:, p % 2, :, 0:n], mt_bank(p)[:, :].rearrange("p (c m) -> p c m", c=CT)[:, :, 0:n],
                        mt_hi[:, p % 2, :, 0:n]).then_inc(mt_has_lo, 1)

            def mem_lo_part(b, p):
                dve.wait_ge(mem_has_hi, MP * b + p + 1)
                ts, raw, r = mem_pair(p)
                lo_part(mem_lo[0:r, ts, :], mem_raw[0:r, raw, :], mem_hi[0:r, ts, :]).then_inc(mem_has_lo, 1)

            def reduce_max(b, first):
                if not first:
                    dve.wait_ge(pe_max_rows, b)
                dve.wait_ge(pe_max_t, b + 1)
                nc.vector.tensor_reduce(col_max[:, :], bank[S_BANK][:, :].rearrange("p (a n) -> p a n", a=NT),
                                        AX.X, ALU.max).then_inc(col_max_done, 1)

            def shift(b, t):
                if t == 0:
                    dve.wait_ge(pe_max_rows, b + 1)
                r = rows(t)
                nc.vector.tensor_tensor(s[0:r, t, :], s[0:r, t, :], bank[MAX_BANK][0:r, :],
                                        ALU.subtract).then_inc(shifted, 1)

            def p_lo_part(b, t):
                dve.wait_ge(p_has_hi, MT * b + t + 1)
                if t >= LO_RING:
                    dve.wait_ge(pe_u, MT * b + t - LO_RING + 1)
                r = rows(t)
                lo_part(p_lo[0:r, t % LO_RING, :], p_tmp[0:r, t % TMP_RING, :], p_hi[0:r, t, :]).then_inc(p_has_lo, 1)

            def softmax(b, t, with_x):
                if t + 3 < MT:
                    shift(b, t + 3)
                if with_x and t in X_AT:
                    xt_lo_part(b + 1, X_AT.index(t))
                p_lo_part(b, t)

            def add_bias(b, j, first):
                dve.wait_ge(pe_gx, NT * b + j + 1)
                if not first:
                    dve.wait_ge(gated, NT * (b - 1) + j + 1)
                nc.vector.tensor_tensor(gate[:, j, :], bank[QX_BANKS[j % 2]][:, :], bias_rows[:, :],
                                        ALU.add).then_inc(gx_done, 1)

            def xt_lo_part(b, k, first=False):
                dve.wait_ge(xt_has_hi, DT * b + k + 1)
                lo_part(xt_lo[:, k, :], x_bank(k, first)[:, :], xt_hi[:, k, :]).then_inc(xt_has_lo, 1)

            def q_lo_part(b, c):
                dve.wait_ge(q_has_hi, CT * b + c + 1)
                lo_part(q_lo[:, c, :], bank[QX_BANKS[c]][:, :], q_hi[:, c, :]).then_inc(q_has_lo, 1)

            def u_lo_part(b, c):
                dve.wait_ge(u_has_hi, CT * b + c + 1)
                lo_part(u_lo[:, c, :], bank[U_BANK + c][:, :], u_hi[:, c, :]).then_inc(u_has_lo, 1)

            def reciprocal(b):
                dve.wait_ge(pe_sum, b + 1)
                nc.vector.reciprocal(r_sum[:, :], bank[MAX_BANK][:, 0:NT]).then_inc(r_first, 1)
                dve.wait_ge(r_first, b + 1)
                nc.vector.tensor_scalar(r_half[:, :], r_sum[:, :], 0.5, None, ALU.mult).then_inc(r_done, 1)

            def gate_input(b, j):
                dve.wait_ge(pe_g, NT * b + j + 1)
                nc.vector.scalar_tensor_tensor(gate[:, j, :], bank[G_BANK + j % 2][:, :], r_sum[:, j : j + 1],
                                               gate[:, j, :], ALU.mult, ALU.add).then_inc(z_done, 1)

            def transpose_x(b, k):
                if k >= 2:
                    dve.wait_ge(xt_has_lo, DT * b + k - 1)
                dve.wait_ge(in_x, 16 * BLOCKS * b)
                nc.vector.transpose(x_bank(k, False)[:, :].rearrange("p (r i) -> p r i", i=BLOCK),
                                    tile_columns(x_blocks, k, DT)).then_inc(xt_done, 1)

            def transpose_mem(b, p):
                if p < 2:
                    dve.wait_ge(in_blocks[0], 16 * BLOCKS * b)
                    if p == 1:
                        dve.wait_ge(xt_has_lo, DT * b + 3)
                else:
                    dve.wait_ge(mt_has_lo, MP * b + p - 1)
                    dve.wait_ge(in_blocks[1], 16 * (BLOCKS + 1) * (b + 1))
                r0, r1 = 2 * p * P // BLOCK, min(2 * (p + 1) * P // BLOCK, ROW_BLOCKS)
                nc.vector.transpose(
                    mt_bank(p)[:, :].rearrange("p (c r i) -> p c r i", c=CT, i=BLOCK)[:, :, 0 : r1 - r0, :],
                    mem_blocks[:, r0:r1, :].rearrange("p r (i c) -> p c r i", i=BLOCK)).then_inc(mt_done, 1)

            def transpose_next(b, t, first):
                if t in X_BLOCKS_AT:
                    if t == X_BLOCKS_AT[0]:
                        if first:
                            dve.wait_ge(wt_split_lo, 8)
                        else:
                            dve.wait_ge(ctx_copied, NT * b)
                    transpose_x(b + 1, X_BLOCKS_AT.index(t))
                if t in MEM_BLOCKS_AT:
                    if t == MEM_BLOCKS_AT[0] and not first:
                        dve.wait_ge(z_done, NT * b)
                    transpose_mem(b + 1, MEM_BLOCKS_AT.index(t))

            def gate_ctx(b, j):
                dve.wait_ge(tanh_done, NT * b + j + 1)
                dve.wait_ge(ctx_copied, NT * b + j + 1)
                nc.vector.scalar_tensor_tensor(fused[:, j, :], gate[:, j, :], 1.0, fused[:, j, :],
                                               ALU.add, ALU.mult).then_inc(gated, 1)

            def add_x(b, j):
                dve.wait_ge(gated, NT * b + j + 1)
                dve.wait_ge(in_x_again[j % 2], 16 * (2 * b + j // 2 + 1))
                nc.vector.tensor_tensor(fused[:, j, :], fused[:, j, :], x_again[:, j % 2, :],
                                        ALU.add).then_inc(fused_done, 1)

            def rms(b):
                count = [NEWTON_OPS * b]

                def link(instruction):
                    count[0] = count[0] + 1
                    instruction.then_inc(newton, 1)
                    dve.wait_ge(newton, count[0])

                dve.wait_ge(squares_done, NT * (b + 1))
                link(nc.vector.tensor_scalar(mean_sq[:, :], sq_sum[:, :], 1.0 / D, EPS, ALU.mult, ALU.add))
                link(nc.vector.tensor_scalar(r_rms[:, :].bitcast(I32), mean_sq[:, :].bitcast(I32), -0.5, RSQRT_MAGIC,
                                             ALU.mult, ALU.add))
                for _ in range(NEWTON_STEPS):
                    link(nc.vector.tensor_tensor(nw_a[:, :], r_rms[:, :], mean_sq[:, :], ALU.mult))
                    link(nc.vector.scalar_tensor_tensor(nw_b[:, :], nw_a[:, :], -0.5, r_rms[:, :], ALU.mult, ALU.mult))
                    link(nc.vector.scalar_tensor_tensor(r_rms[:, :], nw_b[:, :], 1.5, r_rms[:, :], ALU.add, ALU.mult))

            def scale_by_norm(j):
                dve.wait_ge(fused_done, NT * (B - 1) + j + 1)
                nc.vector.tensor_tensor(gate[:, j, :], fused[:, j, :], norm_rows[:, :], ALU.mult).then_inc(normed, 1)

            def output(b, j):
                nc.vector.scalar_tensor_tensor(fused[:, j, :], fused[:, j, :], r_rms[:, j : j + 1], norm_rows[:, :],
                                               ALU.mult, ALU.mult).then_inc(out_done, 1)

            def weights(g):
                dve.wait_ge(wt_split_hi, g + 1)
                if g in WG1T:
                    hi, lo = wg1t_hi[:, g - WG1T[0], :], wg1t_lo[:, g - WG1T[0], :]
                elif g in WT:
                    hi, lo = wt_hi[:, g - WT[0], :], wt_lo[:, g - WT[0], :]
                else:
                    hi, lo = v_hi[:, g - V[0], :], v_lo[:, g - V[0], :]
                lo_part(lo, weight_bank(g)[:, :], hi).then_inc(wt_split_lo, 1)

            def iteration(b, first, last):
                transpose_mem(b, 2)
                for p in range(MP):
                    if p >= 1:
                        running_max(b, 2 * p)
                    if p + 2 < MP:
                        mt_lo_part(b, p + 2)
                    if p + 3 < MP:
                        transpose_mem(b, p + 3)
                    if 2 * p + 1 < MT:
                        running_max(b, 2 * p + 1)
                    for q in SPLIT_BY_SCORES.get(p, []):
                        mem_lo_part(b, q)
                if first:
                    dve.wait_ge(in_rows, 32)
                    reduce_max(b, first)
                    for g in [*WG1T, V[0]]:
                        weights(g)
                    shift(b, 0)
                    shift(b, 1)
                    shift(b, 2)
                    for t in range(MT):
                        for q in SPLIT_BY_SOFTMAX.get(t, []):
                            mem_lo_part(b, q)
                        softmax(b, t, not last)
                        if t == 1:
                            weights(V[1])
                        if 1 <= t < 1 + NT:
                            add_bias(b, t - 1, first)
                        transpose_next(b, t, first)
                else:
                    reciprocal(b - 1)
                    gate_input(b - 1, 0)
                    reduce_max(b, first)
                    gate_ctx(b - 1, 0)
                    gate_input(b - 1, 1)
                    add_x(b - 1, 0)
                    shift(b, 0)
                    shift(b, 1)
                    shift(b, 2)
                    for t in range(MT):
                        if t in (1, 2):
                            gate_input(b - 1, t + 1)
                        if 3 <= t < 3 + NT:
                            add_bias(b, t - 3, first)
                        if t in (0, 2, 4):
                            gate_ctx(b - 1, 1 + t // 2)
                        if t in ADD_AT:
                            add_x(b - 1, ADD_AT.index(t) + 1)
                        for q in SPLIT_BY_SOFTMAX.get(t, []):
                            mem_lo_part(b, q)
                        softmax(b, t, not last)
                        if not last:
                            transpose_next(b, t, first)
                    rms(b - 1)
                    for j in range(NT):
                        output(b - 1, j)
                if not last:
                    q_lo_part(b + 1, 0)
                    q_lo_part(b + 1, 1)
                    mt_lo_part(b + 1, 0)
                    mt_lo_part(b + 1, 1)
                for c in range(CT):
                    u_lo_part(b, c)

            nc.vector.memset(ones[:, :], 1.0).then_inc(ready_ones, 1)
            nc.vector.memset(mem_blocks[:, ROW_BLOCKS - 1, :], 0.0).then_inc(ready_pad, 1)
            dve.wait_ge(w_split_hi, CT)
            for c in range(CT):
                cs = slice(c * P, (c + 1) * P)
                lo_part(w_lo[:, :, cs], tile_columns(w_raw, c, CT), w_hi[:, :, cs]).then_inc(w_split_lo, 1)
            for k in range(DT):
                xt_lo_part(0, k, True)
            mt_lo_part(0, 0)
            weights(WT[0])
            for c in range(CT):
                q_lo_part(0, c)
            mt_lo_part(0, 1)
            weights(WT[1])
            iteration(0, True, False)
            with dve.Fori(1, B - 1) as b:
                iteration(b, False, False)
            iteration(B - 1, False, True)
            reciprocal(B - 1)
            for j in range(NT):
                gate_input(B - 1, j)
                if j >= 1:
                    gate_ctx(B - 1, j - 1)
                    add_x(B - 1, j - 1)
                    if j < NT - 1:
                        scale_by_norm(j - 1)
            gate_ctx(B - 1, NT - 1)
            add_x(B - 1, NT - 1)
            scale_by_norm(NT - 2)
            rms(B - 1)
            nc.vector.tensor_scalar(fused[:, 0, :], gate[:, 0, :], r_rms[:, 0:1], None, ALU.mult).then_inc(out_done, 1)
            output(B - 1, NT - 1)

        @block.gpsimd
        def _(pool):
            def add_p(b, t, first):
                pool.wait_ge(exp_done, MT * b + t + 1)
                r = rows(t)
                if t == 1:
                    if not first:
                        pool.wait_ge(pe_sum, b)
                    a = p_tmp[0:r, 0, :]
                else:
                    pool.wait_ge(p_added, (MT - 1) * b + t - 1)
                    a = psum_rows[0:r, :]
                nc.gpsimd.tensor_tensor(psum_rows[0:r, :], a, p_tmp[0:r, t % TMP_RING, :], ALU.add).then_inc(p_added, 1)

            nc.gpsimd.memset(ident[:, :], 0.0).then_inc(cleared, 1)
            pool.wait_ge(cleared, 1)
            nc.gpsimd.affine_select(out=ident[:, :], in_=ident[:, :], compare_op=ALU.not_equal, fill=1.0, base=0,
                                    pattern=[[-1, P]], channel_multiplier=1).then_inc(ready_ident, 1)
            for t in range(1, MT):
                add_p(0, t, True)
            with pool.Fori(1, B) as b:
                for t in range(1, MT):
                    add_p(b, t, False)


_INS = ["x", "ctx_1024", "L0_xattn_W_mem", "L0_xattn_W_gate", "L0_xattn_b_gate", "L0_xattn_norm_w"]
_OUTS = [((8, 512, 512), "float32")]


def kernel(**inputs):
    import numpy as _np
    import concourse.bacc as _bacc
    from concourse import mybir as _mybir
    from concourse.bass_utils import run_bass_kernel_spmd as _run

    nc = _bacc.Bacc("TRN2", target_bir_lowering=False, num_devices=1, dynamic_dma_scratch_size=1024)
    arrays, args = {}, []
    for name in _INS:
        a = _np.ascontiguousarray(inputs[name])
        arrays[f"in_{name}_dram"] = a
        args.append(nc.dram_tensor(f"in_{name}_dram", a.shape, _mybir.dt.from_np(a.dtype), kind="ExternalInput").ap())
    for i, (shape, dtype) in enumerate(_OUTS):
        dt = _mybir.dt.from_np(_np.dtype(dtype))
        args.append(nc.dram_tensor(f"out_{i}_dram", shape, dt, kind="ExternalOutput").ap())
    xattn_kernel(nc, *args)
    r = _run(nc, [arrays], core_ids=[0])
    return r.results[0]["out_0_dram"]
```
